# Optimizing a Trainium2 kernel written in Bass

```python
import numpy as np
import jax
import jax.numpy as jnp

def _softmax(x, axis=-1):
    return jax.nn.softmax(x, axis=axis)

def _gelu(x):
    return jax.nn.gelu(x, approximate=True)

def _silu(x):
    return jax.nn.silu(x)

def _sigmoid(x):
    return jax.nn.sigmoid(x)

def _layernorm(x, axis=-1, eps=1e-05):
    m = jnp.mean(x, axis=axis, keepdims=True)
    v = jnp.var(x, axis=axis, keepdims=True)
    return (x - m) / jnp.sqrt(v + eps)

def _scatter_add(tgt, idx, src, axis=0):
    return tgt.at[idx].add(src)

def _segment_sum(src, seg, n):
    return jax.ops.segment_sum(src, seg, n)
kernel_name = 'mk_adaln_d1_jaxref_r8_2e1a45'

def setup_inputs(seed: int=0):
    np.random.seed(seed)
    _w = jnp.asarray

    def _L0_attn_setup():
        import jax, jax.numpy as jnp
        import numpy as np
        import math
        NH, NKV, D = (32, 8, 128)

        def _alibi_slopes(n):
            cp2 = 2 ** math.floor(math.log2(n))
            base = 2.0 ** (-8.0 / cp2)
            slopes = base ** np.arange(1, cp2 + 1, dtype=np.float32)
            if cp2 != n:
                extra_base = 2.0 ** (-4.0 / cp2)
                extra = extra_base ** np.arange(1, 1 + 2 * (n - cp2), 2, dtype=np.float32)
                slopes = np.concatenate([slopes, extra])
            return slopes.astype(np.float32)
        key = jax.random.key(seed)
        k1, k2, k3 = jax.random.split(key, 3)
        B, S, H = (4, 128, 512)
        qkv_out = NH * D + 2 * NKV * D
        return {'hidden_states': jax.random.normal(k1, (B, S, H), jnp.float32) * 0.02, 'w_qkv': jax.random.normal(k2, (H, qkv_out), jnp.float32) * 0.02, 'w_o': jax.random.normal(k3, (NH * D, H), jnp.float32) * 0.02}
    _L0_attn_in = _L0_attn_setup()

    def _L0_ffn_setup():
        import jax, jax.numpy as jnp
        import numpy as np
        HIDDEN = 512
        INTER = 1376
        GROUPSIZE = 128
        PACK = 8

        def dequant_gptq(qweight, scales, zeros, groupsize):
            K = qweight.shape[0] * PACK
            N = qweight.shape[1]
            k = jnp.arange(K)
            q = qweight[k // PACK, :] >> (k % PACK * 4)[:, None] & 15
            n = jnp.arange(N)
            z = zeros[:, n // PACK] >> (n % PACK * 4)[None, :] & 15
            s = scales.astype(jnp.float32)
            zp = (z.astype(jnp.float32) + 1.0) * s
            g = k // groupsize
            return q.astype(jnp.float32) * s[g] - zp[g]
        key = jax.random.key(seed)
        ks = jax.random.split(key, 11)
        imax = 2147483647
        G_h = HIDDEN // GROUPSIZE
        G_i = (INTER + GROUPSIZE - 1) // GROUPSIZE
        x = (jax.random.normal(ks[0], (2, 256, HIDDEN), dtype=jnp.float32) * 0.5).astype(jnp.float16)
        return {'x': x, 'gate_qweight': jax.random.randint(ks[1], (HIDDEN // PACK, INTER), 0, imax, dtype=jnp.int32), 'gate_scales': (jax.random.uniform(ks[2], (G_h, INTER), dtype=jnp.float32) * 0.01 + 0.001).astype(jnp.float16), 'gate_zeros': jax.random.randint(ks[3], (G_h, INTER // PACK), 0, imax, dtype=jnp.int32), 'up_qweight': jax.random.randint(ks[4], (HIDDEN // PACK, INTER), 0, imax, dtype=jnp.int32), 'up_scales': (jax.random.uniform(ks[5], (G_h, INTER), dtype=jnp.float32) * 0.01 + 0.001).astype(jnp.float16), 'up_zeros': jax.random.randint(ks[6], (G_h, INTER // PACK), 0, imax, dtype=jnp.int32), 'down_qweight': jax.random.randint(ks[7], (INTER // PACK, HIDDEN), 0, imax, dtype=jnp.int32), 'down_scales': (jax.random.uniform(ks[8], (G_i, HIDDEN), dtype=jnp.float32) * 0.01 + 0.001).astype(jnp.float16), 'down_zeros': jax.random.randint(ks[9], (G_i, HIDDEN // PACK), 0, imax, dtype=jnp.int32)}
    _L0_ffn_in = _L0_ffn_setup()
    _L0_c = _w((lambda *s: np.random.randn(*s).astype(np.float32) * 0.05)(1, 512))
    _L0_wmod = _w((lambda *s: np.random.randn(*s).astype(np.float32) * 0.05)(512, 6 * 512) * 512 ** (-0.5))
    _d = {'L0_attn_hidden_states': _L0_attn_in['hidden_states'], 'L0_attn_w_qkv': _L0_attn_in['w_qkv'], 'L0_attn_w_o': _L0_attn_in['w_o'], 'L0_ffn_gate_qweight': _L0_ffn_in['gate_qweight'], 'L0_ffn_gate_scales': _L0_ffn_in['gate_scales'], 'L0_ffn_gate_zeros': _L0_ffn_in['gate_zeros'], 'L0_ffn_up_qweight': _L0_ffn_in['up_qweight'], 'L0_ffn_up_scales': _L0_ffn_in['up_scales'], 'L0_ffn_up_zeros': _L0_ffn_in['up_zeros'], 'L0_ffn_down_qweight': _L0_ffn_in['down_qweight'], 'L0_ffn_down_scales': _L0_ffn_in['down_scales'], 'L0_ffn_down_zeros': _L0_ffn_in['down_zeros'], 'L0_c': _L0_c, 'L0_wmod': _L0_wmod}
    _x0 = _d['L0_attn_hidden_states']
    _d['L0_attn_hidden_states'] = jax.random.normal(jax.random.fold_in(jax.random.key(seed), 1), (1, 1024, 512), dtype=_x0.dtype)
    del _x0
    return _d

def reference(L0_attn_hidden_states, L0_attn_w_qkv, L0_attn_w_o, L0_ffn_gate_qweight, L0_ffn_gate_scales, L0_ffn_gate_zeros, L0_ffn_up_qweight, L0_ffn_up_scales, L0_ffn_up_zeros, L0_ffn_down_qweight, L0_ffn_down_scales, L0_ffn_down_zeros, L0_c, L0_wmod):

    def _L0_attn_ref(hidden_states, w_qkv, w_o):
        import jax, jax.numpy as jnp
        import numpy as np
        import math
        NH, NKV, D = (32, 8, 128)

        def _alibi_slopes(n):
            cp2 = 2 ** math.floor(math.log2(n))
            base = 2.0 ** (-8.0 / cp2)
            slopes = base ** np.arange(1, cp2 + 1, dtype=np.float32)
            if cp2 != n:
                extra_base = 2.0 ** (-4.0 / cp2)
                extra = extra_base ** np.arange(1, 1 + 2 * (n - cp2), 2, dtype=np.float32)
                slopes = np.concatenate([slopes, extra])
            return slopes.astype(np.float32)
        B, S, H = hidden_states.shape
        G = NH // NKV
        scale = D ** (-0.5)
        qkv = hidden_states @ w_qkv
        q = qkv[..., :NH * D].reshape(B, S, NKV, G, D)
        k = qkv[..., NH * D:NH * D + NKV * D].reshape(B, S, NKV, D)
        v = qkv[..., NH * D + NKV * D:].reshape(B, S, NKV, D)
        scores = jnp.einsum('bqhgd,bkhd->bhgqk', q, k) * scale
        slopes = jnp.asarray(_alibi_slopes(NH)).reshape(NKV, G)
        pos = jnp.arange(S)
        rel = pos[:, None] - pos[None, :]
        sqrt_dist = jnp.sqrt(jnp.maximum(rel, 0).astype(jnp.float32))
        bias = -slopes[:, :, None, None] * sqrt_dist
        bias = jnp.where(rel[None, None] >= 0, bias, -jnp.inf)
        attn = jax.nn.softmax(scores + bias[None], axis=-1)
        out = jnp.einsum('bhgqk,bkhd->bqhgd', attn, v).reshape(B, S, NH * D)
        return out @ w_o

    def _L0_ffn_ref(x, gate_qweight, gate_scales, gate_zeros, up_qweight, up_scales, up_zeros, down_qweight, down_scales, down_zeros):
        import jax, jax.numpy as jnp
        import numpy as np
        HIDDEN = 512
        INTER = 1376
        GROUPSIZE = 128
        PACK = 8

        def dequant_gptq(qweight, scales, zeros, groupsize):
            K = qweight.shape[0] * PACK
            N = qweight.shape[1]
            k = jnp.arange(K)
            q = qweight[k // PACK, :] >> (k % PACK * 4)[:, None] & 15
            n = jnp.arange(N)
            z = zeros[:, n // PACK] >> (n % PACK * 4)[None, :] & 15
            s = scales.astype(jnp.float32)
            zp = (z.astype(jnp.float32) + 1.0) * s
            g = k // groupsize
            return q.astype(jnp.float32) * s[g] - zp[g]
        B, S, H = x.shape
        x2 = x.reshape(-1, H).astype(jnp.float32)
        Wg = dequant_gptq(gate_qweight, gate_scales, gate_zeros, GROUPSIZE)
        Wu = dequant_gptq(up_qweight, up_scales, up_zeros, GROUPSIZE)
        Wd = dequant_gptq(down_qweight, down_scales, down_zeros, GROUPSIZE)
        gate = x2 @ Wg
        up = x2 @ Wu
        inter = gate * jax.nn.sigmoid(gate) * up
        out = (inter @ Wd).astype(jnp.float16)
        return out.reshape(B, S, H)
    x = L0_attn_hidden_states
    mod = (_silu(L0_c) @ L0_wmod).reshape(L0_c.shape[0], 6, 1, -1)
    sa, ca, ga, sb, cb, gb = (mod[:, 0], mod[:, 1], mod[:, 2], mod[:, 3], mod[:, 4], mod[:, 5])
    ga = (2 * (ga >= 0) - 1) * jnp.maximum(jnp.abs(ga), 0.25)
    gb = (2 * (gb >= 0) - 1) * jnp.maximum(jnp.abs(gb), 0.25)
    h = _layernorm(x, axis=-1) * (1 + ca) + sa
    x = x + ga * _L0_attn_ref(h, L0_attn_w_qkv, L0_attn_w_o)
    h = _layernorm(x, axis=-1) * (1 + cb) + sb
    x = x + gb * _L0_ffn_ref(h, L0_ffn_gate_qweight, L0_ffn_gate_scales, L0_ffn_gate_zeros, L0_ffn_up_qweight, L0_ffn_up_scales, L0_ffn_up_zeros, L0_ffn_down_qweight, L0_ffn_down_scales, L0_ffn_down_zeros)
    return x

_drawn_inputs = setup_inputs


def setup_inputs(seed=0):
    import zlib

    import numpy as np

    out = dict(_drawn_inputs(seed))
    spreads = {}
    factors = {'L0_attn_w_qkv': 2.827, 'L0_attn_w_o': 2.807}
    for name, (base, spread) in spreads.items():
        noise = np.random.default_rng([zlib.crc32(name.encode()), seed]).standard_normal(out[name].shape)
        drawn = base * np.exp(spread * noise) if base else spread * noise
        out[name] = jnp.asarray(drawn.astype(out[name].dtype))
    for name, factor in factors.items():
        out[name] = (out[name] * factor).astype(out[name].dtype)
    return out
```

```python
import numpy as np
import concourse.bass as bass
from concourse import mybir

F32 = mybir.dt.float32
F32R = mybir.dt.float32r
F16 = mybir.dt.float16
I32 = mybir.dt.int32
ALU = mybir.AluOpType
ACT = mybir.ActivationFunctionType

P = 128
S = 1024
H = 512
NH, NKV, D = 32, 8, 128
G = NH // NKV
NT = S // P
KT = H // P
HALF = 512
INTER = 1376
PACK = 8
NC_FULL, C_LAST = INTER // P, INTER % P
NCH = NC_FULL + 1
ROWS = P // PACK
MASKED = 1.0e30
EPS = 1e-5

PAIRS = NKV // 2
UNITS = 2 * NT
BLOCKS = NT * (NT + 1)

A, B = 0, 1
USES = ([("k", A, 0), ("v", A, 0), ("v", B, 0)] + [("q", A, g) for g in range(G)]
        + [("q", A, g) for g in range(G)] + [("q", B, g) for g in range(G)] + [("k", B, 0)]
        + [("q", B, g) for g in range(G)])
NU = len(USES)
RING = 4
USE_QA1, USE_QB0, USE_KB, USE_QB1 = 7, 11, 15, 16
HEAD_GROUPS = ([("k", A, 0, h) for h in range(2)] + [("v", A, t, 0) for t in range(NT)]
               + [("q", A, g, 0) for g in range(G)])
FILL = {}
for _i in range(G):
    FILL[(A, _i)] = [(0, ("q", A, _i, 1), USE_QA1 + _i)]
    FILL[(A, G + _i)] = [(0, ("q", B, _i, 0), USE_QB0 + _i)]
    FILL[(B, _i)] = [(0, ("q", B, _i, 1), USE_QB1 + _i)]
FILL[(A, NT - 1)] += [(1, ("k", B, 0, 0), USE_KB), (2, ("k", B, 0, 1), USE_KB)]
GROUPS = HEAD_GROUPS + [f[1] for hd in range(2) for i in range(NT) for f in FILL.get((hd, i), [])]
NG = len(GROUPS)


LAST_GROUP = []
for _u, (_k, _hd, _g) in enumerate(USES):
    _of = [n for n, (k, hd, m, half) in enumerate(GROUPS)
           if k == _k and (k == "v" or hd == _hd) and (k != "q" or m == _g)]
    if _k == "q":
        _of = [_of[0 if _u in range(3, USE_QA1) or _u in range(USE_QB0, USE_KB) else 1]]
    LAST_GROUP.append(max(_of))


def group_index(kind, hd, n, half):
    return GROUPS.index((kind, hd, n, half))


def block_index(hd, i, s):
    return hd * (BLOCKS // 2) + i * (i + 1) // 2 + s


def score_slots(hd, i):
    if hd == A and i == NT - 1:
        return [3, 4, 5, 6]
    return {0: [0, 0, 1, 1], 1: [0, 0, 1, 2]}.get(i, [0, 1, 2, 3])


def wo_slot(hd, i):
    return 3 if (hd, i) == (A, NT - 1) else 1


def next_unit(hd, i):
    if i + 1 < NT:
        return hd, i + 1
    return (B, 0) if hd == A else None


def score_banks(i):
    n = (i + 1) * P
    return [max(256, min(n, 512))] + ([max(256, n - 512)] if n > 512 else [])


def build(nc, x_in, w_qkv, w_o, qw, sc, zr, c_in, w_mod, sqrt_dist, head_table, ident_in, shift_in, out):
    at = [((nc.sbuf_base if not callable(nc.sbuf_base) else nc.sbuf_base()) + 63) // 64 * 64]

    def place(name, shape, dtype, offset=None):
        size = int(np.prod(shape[1:])) * mybir.dt.size(dtype)
        where = at[0] if offset is None else offset
        if offset is None:
            at[0] += (size + 31) // 32 * 32
        return nc.alloc_sbuf_tensor_at(name, shape, dtype, offset=where)

    x = place("x", [P, NT, H], F32)
    h_hi = place("h_hi", [P, KT, S], F32R)
    h_lo = place("h_lo", [P, KT, S], F32R)
    ident = place("ident", [P, P], F32)
    gate_b = place("gate_b", [P, H], F32)
    mod_cols = place("mod_cols", [P, 4, KT], F32)
    stats = place("stats", [P, NT, 6], F32)
    moments = place("moments", [P, NT, 2], F32)
    std = place("std", [P, NT], F32)
    rstd = place("rstd", [P, NT], F32)
    eps_col = place("eps_col", [P, 1], F32)
    base = at[0]

    q_hi = place("q_hi", [P, G, S], F32R)
    q_lo = place("q_lo", [P, G, S], F32R)
    k_hi = place("k_hi", [P, S], F32R)
    k_lo = place("k_lo", [P, S], F32R)
    v_hi = place("v_hi", [P, 2, NT, D], F32R)
    v_lo = place("v_lo", [P, 2, NT, D], F32R)
    probs = place("probs", [P, 2, G, S], F32)
    pt_hi = place("pt_hi", [P, 2, G * P], F32R)
    pt_lo = place("pt_lo", [P, 2, G * P], F32R)
    o_hi = place("o_hi", [P, G * P], F32R)
    o_lo = place("o_lo", [P, G * P], F32R)
    w_raw = place("w_raw", [P, RING, KT, P], F32)
    w_hi = place("w_hi", [P, RING, KT, P], F32R)
    w_lo = place("w_lo", [P, RING, KT, P], F32R)
    wo_raw = place("wo_raw", [P, G, H], F32)
    wo_hi = place("wo_hi", [P, G, H], F32R)
    wo_lo = place("wo_lo", [P, G, H], F32R)
    sdist = place("sdist", [P, S], F32)
    gate_a = place("gate_a", [P, H], F32)
    table = place("table", [P, PAIRS, 3, 2, G], F32)
    consts = place("consts", [P, 3, 2, G], F32)
    low = place("low", [P, 2, G], F32)
    shift = place("shift", [P, 2, G], F32)
    rowsum = place("rowsum", [P, 2, G], F32)
    inv = place("inv", [P, 2, G], F32)
    assert at[0] <= (nc.sbuf_usable_end() if callable(nc.sbuf_usable_end) else nc.sbuf_usable_end), at[0]

    at[0] = base
    wmod = place("wmod", [P, 6, KT, H], F32)
    xn = place("xn", [P, 2, H], F32)
    ln_f = place("ln_f", [P, 2, HALF], F32)
    c_col = place("c_col", [P, KT], F32)
    c_tmp = place("c_tmp", [P, 3, KT], F32)
    silu_c = place("silu_c", [P, KT], F32)
    silu_b = place("silu_b", [P, KT, P], F32)
    g_tmp = place("g_tmp", [P, 2, 2, H], F32)

    at[0] = base
    t_hi = place("t_hi", [P, NCH, S], F32R)
    t_lo = place("t_lo", [P, NCH, S], F32R)
    xn2 = place("xn2", [P, 2, H], F32, base)
    ln_f2 = place("ln_f2", [P, 2, HALF], F32, base + 2 * H * 4)
    q4 = place("q4", [P, 2, 2, KT, P], I32)
    s4 = place("s4", [P, 2, 2, KT, P], F16)
    z4 = place("z4", [P, 2, 2, KT, P // PACK], I32)
    nib = place("nib", [P, KT * P], I32)
    znib = place("znib", [P, 2, KT * P], I32)
    dif = place("dif", [P, KT * P], F32)
    wf = place("wf", [P, 2, KT * P], F32)
    gu_hi = place("gu_hi", [P, 2, 2, KT, P], F32R)
    gu_lo = place("gu_lo", [P, 2, 2, KT, P], F32R)
    sig = place("sig", [P, HALF], F32)
    act1 = place("act1", [P, HALF], F32)
    act2_at = at[0]
    act2 = place("act2", [P, 2, HALF], F32)
    shifts = place("shifts", [P, 1 + PACK], I32)
    qd = place("qd", [P, 2, H], I32)
    sd = place("sd", [P, 2, H], F16)
    zd = place("zd", [P, 2, H // PACK], I32)
    d_hi = place("d_hi", [P, 2, H], F32R)
    d_lo = place("d_lo", [P, 2, H], F32R)
    o16 = place("o16", [P, 2, H], F16)
    fin = place("fin", [P, 2, H], F32, act2_at)
    assert at[0] <= (nc.sbuf_usable_end() if callable(nc.sbuf_usable_end) else nc.sbuf_usable_end), at[0]

    ps = nc.alloc_psum_tensor("ps", [P, 8, 512], F32)
    T_BANK, O_BANK, M_BANK = 4, 6, 7

    def r32(ap):
        return ap.bitcast(F32)

    sem = lambda name: nc.alloc_semaphore(name)
    waits_passed = sem("waits_passed")
    x_in_sem = [sem(f"x_loaded{t}") for t in range(NT)]
    c_loaded = sem("c_loaded")
    consts_loaded = sem("consts_loaded")
    mod_loaded = [sem(f"mod_loaded{m}") for m in range(6)]
    silu_step = sem("silu_step")
    silu_exp = sem("silu_exp")
    silu_ready = sem("silu_ready")
    mod_done = sem("mod_done")
    mod_ready = sem("mod_ready")
    gate_step = sem("gate_step")
    stat_step = sem("stat_step")
    var_ready = sem("var_ready")
    std_ready = sem("std_ready")
    xn_ready = sem("xn_ready")
    xn_moved = sem("xn_moved")
    ln_hi_done = sem("ln_hi_done")
    ln_f_step = sem("ln_f_step")
    h_ready = sem("h_ready")
    w_loaded = [sem(f"w_loaded{i}") for i in range(RING)]
    w_hi_done = sem("w_hi_done")
    w_ready = sem("w_ready")
    wo_loaded = sem("wo_loaded")
    wo_scaled = sem("wo_scaled")
    wo_hi_done = sem("wo_hi_done")
    wo_ready = sem("wo_ready")
    head_consts = sem("head_consts")
    proj_done = sem("proj_done")
    proj_hi = sem("proj_hi")
    proj_split = sem("proj_split")
    s_done = sem("s_done")
    s_biased = sem("s_biased")
    shift_ready = sem("shift_ready")
    exp_done = sem("exp_done")
    inv_ready = sem("inv_ready")
    normed = sem("normed")
    t_done = sem("t_done")
    pt_hi_done = sem("pt_hi_done")
    pt_split = sem("pt_split")
    pv_done = sem("pv_done")
    o_hi_done = sem("o_hi_done")
    o_split = sem("o_split")
    y_done = sem("y_done")
    x_added = sem("x_added")
    shifts_loaded = sem("shifts_loaded")
    gu_loaded = [sem(f"gu_loaded{i}") for i in range(2)]
    dq_step = sem("dq_step")
    wf_ready = sem("wf_ready")
    wf_hi = sem("wf_hi")
    wf_split = sem("wf_split")
    gate_done = sem("gate_done")
    up_done = sem("up_done")
    sig_done = sem("sig_done")
    silu_done = sem("silu_done")
    act_ready = sem("act_ready")
    act_hi = sem("act_hi")
    act_split = sem("act_split")
    d_loaded = [sem(f"d_loaded{i}") for i in range(2)]
    d_used = sem("d_used")
    y2_done = sem("y2_done")
    o16_done = sem("o16_done")
    fin_step = sem("fin_step")
    fin_ready = sem("fin_ready")
    out_stored = [sem(f"out_stored{i}") for i in range(2)]

    def alone(eng):
        eng.sem_inc(waits_passed, 1)

    W3 = w_qkv.rearrange("(k p) n -> p k n", p=P)

    def use_columns(u, it):
        kind, hd, g = USES[u]
        if kind == "q":
            return it * (2 * G * D) + (hd * G + g) * D
        return it * (2 * D) + (NH * D + (NKV * D if kind == "v" else 0) + hd * D)

    LN_BANK = lambda half, f: half * KT + f

    block = nc.Block()
    with block:

        @block.sync
        def _(sp):
            for t in range(NT):
                sp.dma_start(x[:, t, :], x_in[t * P:(t + 1) * P, :]).then_inc(x_in_sem[t], 16)
            sp.dma_start(ident[:, :], ident_in).then_inc(consts_loaded, 16)
            sp.dma_start(table[:, :, :, :, :], head_table).then_inc(consts_loaded, 16)
            sp.dma_start(sdist[:, :], sqrt_dist).then_inc(consts_loaded, 16)
            with sp.Fori(0, PAIRS) as it:
                def load_wo(hd):
                    sp.wait_ge(wo_ready, (it * 2 + hd) * G + 1)
                    alone(sp)
                    rows = bass.ds(it * (2 * G * D) + hd * G * D, G * D)
                    sp.dma_start(wo_raw[:, :, :], w_o[rows, :].rearrange("(g p) n -> p g n", p=P)
                                 ).then_inc(wo_loaded, 16)

                for u in range(NU):
                    slot = u % RING
                    sp.wait_ge(w_ready, it * NU + (u + 1))
                    alone(sp)
                    sp.dma_start(w_raw[:, slot, :, :], W3[:, :, bass.ds(use_columns(u, it), P)]
                                 ).then_inc(w_loaded[slot], 16)
                    if u == 2:
                        load_wo(A)
                    if u == USE_QA1 + G:
                        load_wo(B)
            sp.wait_ge(x_added, PAIRS * UNITS + 1)
            sp.wait_ge(y_done, PAIRS * UNITS + 1)
            sp.dma_start(shifts[:, :], shift_in).then_inc(shifts_loaded, 16)

            def load_gu(c, par, width, count):
                sp.wait_ge(wf_ready, count)
                alone(sp)
                for m in range(2):
                    cols = bass.ds(c * P, width)
                    for k in range(KT):
                        src = qw[m][k * ROWS:(k + 1) * ROWS, cols]
                        sp.dma_start(q4[:, par, m, k, 0:width],
                                     src.unsqueeze(1).to_broadcast([ROWS, PACK, width])
                                     ).then_inc(gu_loaded[par], 16)
                    sp.dma_start(s4[:, par, m, :, 0:width],
                                 sc[m][:, cols].unsqueeze(0).to_broadcast([P, KT, width])
                                 ).then_inc(gu_loaded[par], 16)
                    sp.dma_start(z4[:, par, m, :, 0:width // PACK],
                                 zr[m][:, bass.ds(c * (P // PACK), width // PACK)].unsqueeze(0)
                                 .to_broadcast([P, KT, width // PACK])).then_inc(gu_loaded[par], 16)

            with sp.Fori(0, NC_FULL // 2) as it:
                for par in range(2):
                    load_gu(it * 2 + par, par, P, it * 4 + (2 * par + 2))
            load_gu(NC_FULL, 0, C_LAST, 2 * NC_FULL + 2)

            def load_down(c):
                par, rows = c % 2, (ROWS if c < NC_FULL else C_LAST // PACK)
                sp.dma_start(qd[0:rows * PACK, par, :],
                             qw[2][c * ROWS:c * ROWS + rows, :].unsqueeze(1).to_broadcast([rows, PACK, H])
                             ).then_inc(d_loaded[par], 16)
                sp.dma_start(sd[:, par, :], sc[2][c:c + 1, :].to_broadcast([P, H])
                             ).then_inc(d_loaded[par], 16)
                sp.dma_start(zd[:, par, :], zr[2][c:c + 1, :].to_broadcast([P, H // PACK])
                             ).then_inc(d_loaded[par], 16)

            for c in range(NCH):
                if c >= 2:
                    sp.wait_ge(wf_ready, 4 + 2 * NCH + (c - 1))
                load_down(c)
            for t in range(NT):
                sp.wait_ge(fin_ready, t + 1)
                sp.dma_start(out[t * P:(t + 1) * P, :], fin[:, t % 2, :]).then_inc(out_stored[t % 2], 16)
            for i in range(2):
                sp.wait_ge(out_stored[i], 16 * (NT // 2))

        @block.gpsimd
        def _(pool):
            pool.sem_inc(w_ready, RING)

            with pool.Fori(0, PAIRS) as it:
                def scale_wo(hd, g):
                    pool.wait_ge(wo_loaded, it * 32 + (hd + 1) * 16)
                    pool.tensor_tensor(wo_raw[:, g, :], wo_raw[:, g, :], gate_a[:, :], ALU.mult
                                       ).then_inc(wo_scaled, 1)

                def split_use(u):
                    slot = u % RING
                    pool.wait_ge(w_loaded[slot], it * (NU // RING * 16) + (u // RING + 1) * 16)
                    pool.wait_ge(proj_done, it * NG + (LAST_GROUP[u - RING] + 2 if u >= RING else 1))
                    alone(pool)
                    pool.tensor_scalar(w_hi[:, slot, :, :], w_raw[:, slot, :, :], 1.0, 1.0, ALU.mult, ALU.mult
                                       ).then_inc(w_hi_done, 1)
                    pool.wait_ge(w_hi_done, it * NU + (u + 1))
                    pool.tensor_tensor(w_lo[:, slot, :, :], w_raw[:, slot, :, :], r32(w_hi[:, slot, :, :]),
                                       ALU.subtract).then_inc(w_ready, 1)

                def normalise(hd, i, g):
                    pool.wait_ge(inv_ready, it * (UNITS * G) + ((hd * NT + i) * G + g + 1))
                    alone(pool)
                    rows = probs[:, i % 2, g, 0:(i + 1) * P]
                    pool.tensor_scalar(rows, rows, inv[:, i % 2, g:g + 1], 1.0, ALU.mult, ALU.mult
                                       ).then_inc(normed, 1)

                for u in range(USE_QA1):
                    split_use(u)
                pool.wait_ge(mod_ready, 2)
                for g in range(G):
                    scale_wo(A, g)
                split_use(USE_QA1)
                for g in range(G):
                    normalise(A, 0, g)
                for hd in range(2):
                    for i in range(NT):
                        nxt = next_unit(hd, i)
                        if nxt:
                            for u in sorted({f[2] for f in FILL.get(nxt, [])}):
                                split_use(u)
                            for g in range(G):
                                normalise(*nxt, g)
                        if hd == A and i >= G:
                            scale_wo(B, i - G)

            def lo_weights(n, m, par, width):
                pool.wait_ge(wf_hi, n + 1)
                pool.tensor_tensor(gu_lo[:, par, m, :, 0:width],
                                   wf[:, m, 0:KT * width].rearrange("p (k n) -> p k n", k=KT),
                                   r32(gu_hi[:, par, m, :, 0:width]), ALU.subtract).then_inc(wf_split, 1)

            def lo_activation(n, c, half, width):
                pool.wait_ge(act_hi, n + 1)
                tok = slice(half * HALF, (half + 1) * HALF)
                pool.tensor_tensor(t_lo[0:width, c, tok], act2[0:width, half, :], r32(t_hi[0:width, c, tok]),
                                   ALU.subtract).then_inc(act_split, 1)

            def ffn_chunk(c, par, width, following):
                if following:
                    for m in range(2):
                        lo_weights((c + 1) * 2 + m, m, 1 - par, following)
                for half in range(2):
                    lo_activation(c * 2 + half, c, half, width)

            for m in range(2):
                lo_weights(m, m, 0, P)
            for c in range(NC_FULL):
                ffn_chunk(c, c % 2, P, P if c + 1 < NC_FULL else C_LAST)
            ffn_chunk(NC_FULL, 0, C_LAST, 0)
            for c in range(NCH):
                n = P if c < NC_FULL else C_LAST
                pool.wait_ge(wf_hi, 2 * NCH + c + 1)
                pool.tensor_tensor(d_lo[0:n, c % 2, :], wf[0:n, c % 2, :], r32(d_hi[0:n, c % 2, :]),
                                   ALU.subtract).then_inc(wf_split, 1)

        @block.scalar
        def _(act):
            act.dma_start(c_col[:, :], c_in).then_inc(c_loaded, 16)
            wm = w_mod.rearrange("(k p) (m n) -> p m k n", p=P, m=6)
            for m in (1, 0, 2, 4, 3, 5):
                act.dma_start(wmod[:, m, :, :], wm[:, m, :, :]).then_inc(mod_loaded[m], 16)
            act.wait_ge(c_loaded, 16)
            nc.scalar.activation(c_tmp[:, 0, :], c_col[:, :], ACT.Exp, scale=-1.0).then_inc(silu_exp, 1)

            def layer_norm(n, scale_col, bias_col):
                act.wait_ge(var_ready, n + 1)
                nc.scalar.activation(std[:, :], moments[:, :, 1], ACT.Sqrt, bias=eps_col[:, 0:1]
                                     ).then_inc(std_ready, 1)
                for half in range(2):
                    act.wait_ge(xn_moved, n * NT + (half + 1) * (NT // 2))
                    for f in range(KT):
                        nc.scalar.activation(h_hi[:, f, half * HALF:(half + 1) * HALF],
                                             ps[:, LN_BANK(half, f), :], ACT.Identity,
                                             scale=mod_cols[:, scale_col, f:f + 1],
                                             bias=mod_cols[:, bias_col, f:f + 1]).then_inc(ln_hi_done, 1)

            act.wait_ge(mod_ready, 1)
            layer_norm(0, 0, 1)

            with act.Fori(0, PAIRS) as it:
                def project_hi(kind, hd, n, half):
                    G_i = group_index(kind, hd, n, half)
                    act.wait_ge(proj_done, it * NG + (G_i + 2))
                    bank = ps[:, G_i % 4 if G_i < len(HEAD_GROUPS) else M_BANK, :]
                    tok = slice(half * HALF, (half + 1) * HALF)
                    if kind == "q":
                        ins = nc.scalar.activation(q_hi[:, n, tok], bank, ACT.Copy,
                                                   scale=consts[:, 0, hd, n:n + 1])
                    elif kind == "k":
                        ins = nc.scalar.activation(k_hi[:, tok], bank, ACT.Copy)
                    else:
                        ins = nc.scalar.activation(v_hi[:, :, n, :],
                                                   bank[:, 0:2 * D].rearrange("p (a d) -> p a d", a=2), ACT.Copy)
                    ins.then_inc(proj_hi, 1)

                def exponential(hd, i, g):
                    n = (hd * NT + i) * G + g
                    act.wait_ge(shift_ready, it * (UNITS * G) + (n + 1))
                    rows = probs[:, i % 2, g, 0:(i + 1) * P]
                    nc.scalar.activation(rows, rows, ACT.Exp, scale=consts[:, 2, hd, g:g + 1],
                                         bias=shift[:, i % 2, g:g + 1],
                                         accum_out=rowsum[:, i % 2, g:g + 1]).then_inc(exp_done, 1)

                act.wait_ge(head_consts, it + 1)
                for grp in HEAD_GROUPS:
                    project_hi(*grp)
                for g in range(G):
                    exponential(A, 0, g)
                for hd in range(2):
                    for i in range(NT):
                        nxt = next_unit(hd, i)
                        waiting = []
                        for s in range(i + 2):
                            if s <= i:
                                b = block_index(hd, i, s)
                                act.wait_ge(t_done, it * BLOCKS + (b + 2))
                                act.wait_ge(pv_done, it * BLOCKS + (b + 1))
                                nc.scalar.activation(pt_hi[:, b % 2, :], ps[:, T_BANK + b % 2, :], ACT.Copy
                                                     ).then_inc(pt_hi_done, 1)
                            for g in waiting:
                                exponential(*nxt, g)
                            waiting = []
                            for slot, grp, _u in FILL.get((hd, i), []):
                                if slot == s:
                                    project_hi(*grp)
                            if nxt:
                                waiting = [g for g in range(G) if score_slots(hd, i)[g] == s]
                        for g in waiting:
                            exponential(*nxt, g)
                        if i == 0:
                            act.wait_ge(y_done, it * UNITS + hd * NT + 1)
                            for g in range(G):
                                act.wait_ge(wo_scaled, it * (2 * G) + (hd * G + g + 1))
                                nc.scalar.activation(wo_hi[:, g, :], wo_raw[:, g, :], ACT.Copy
                                                     ).then_inc(wo_hi_done, 1)
                        n = hd * NT + i
                        act.wait_ge(pv_done, it * BLOCKS + (block_index(hd, i, i) + 3))
                        act.wait_ge(y_done, it * UNITS + (n + 1))
                        nc.scalar.activation(o_hi[:, :], ps[:, O_BANK, :], ACT.Copy).then_inc(o_hi_done, 1)

            layer_norm(1, 2, 3)

            def hi_weights(n, m, par, width):
                act.wait_ge(wf_ready, n + 5)
                if n >= 4:
                    act.wait_ge(up_done, n // 2 * 2 - 2)
                nc.scalar.activation(gu_hi[:, par, m, :, 0:width],
                                     wf[:, m, 0:KT * width].rearrange("p (k n) -> p k n", k=KT), ACT.Copy
                                     ).then_inc(wf_hi, 1)

            def ffn_chunk(c, par, width, following):
                for half in range(2):
                    n = c * 2 + half
                    act.wait_ge(gate_done, n + 1)
                    if n >= 1:
                        act.wait_ge(silu_done, n)
                    nc.scalar.activation(sig[0:width, :], ps[0:width, 2 * (n % 4), :], ACT.Sigmoid
                                         ).then_inc(sig_done, 1)
                    if half == 0 and following:
                        for m in range(2):
                            hi_weights((c + 1) * 2 + m, m, 1 - par, following)
                    act.wait_ge(act_ready, n + 1)
                    nc.scalar.activation(t_hi[0:width, c, half * HALF:(half + 1) * HALF],
                                         act2[0:width, half, :], ACT.Copy).then_inc(act_hi, 1)

            for m in range(2):
                hi_weights(m, m, 0, P)
            for c in range(NC_FULL):
                ffn_chunk(c, c % 2, P, P if c + 1 < NC_FULL else C_LAST)
            ffn_chunk(NC_FULL, 0, C_LAST, 0)
            for c in range(NCH):
                n = P if c < NC_FULL else C_LAST
                act.wait_ge(wf_ready, 4 + 2 * NCH + c + 1)
                if c >= 2:
                    act.wait_ge(d_used, c - 1)
                nc.scalar.activation(d_hi[0:n, c % 2, :], wf[0:n, c % 2, :], ACT.Copy).then_inc(wf_hi, 1)
            for t in range(NT):
                act.wait_ge(y2_done, t + 1)
                if t >= 2:
                    act.wait_ge(fin_step, t - 1)
                nc.scalar.activation(o16[:, t % 2, :], ps[:, t, :], ACT.Copy).then_inc(o16_done, 1)

        @block.vector
        def _(dve):
            dve.sem_inc(wo_ready, 1)
            dve.sem_inc(proj_split, 1)
            dve.sem_inc(s_biased, 2)
            dve.sem_inc(pt_split, 2)
            dve.sem_inc(o_split, 1)
            dve.sem_inc(x_added, 1)
            dve.sem_inc(wf_ready, 4)
            dve.memset(eps_col[:, :], EPS).then_inc(silu_step, 1)

            dve.wait_ge(silu_exp, 1)
            dve.tensor_scalar(c_tmp[:, 1, :], c_tmp[:, 0, :], 1.0, None, ALU.add).then_inc(silu_step, 1)
            dve.wait_ge(silu_step, 2)
            dve.reciprocal(c_tmp[:, 2, :], c_tmp[:, 1, :]).then_inc(silu_step, 1)
            dve.wait_ge(silu_step, 3)
            dve.tensor_tensor(silu_c[:, :], c_col[:, :], c_tmp[:, 2, :], ALU.mult).then_inc(silu_step, 1)
            dve.wait_ge(silu_step, 4)
            dve.tensor_copy(silu_b[:, :, :], silu_c[:, :].unsqueeze(2).to_broadcast([P, KT, P])
                            ).then_inc(silu_ready, 1)

            def statistics(n):
                for t in range(NT):
                    if n == 0:
                        dve.wait_ge(x_in_sem[t], 16)
                    dve.bn_stats(stats[:, t, :], x[:, t, :]).then_inc(stat_step, 1)
                for t in range(NT):
                    dve.wait_ge(stat_step, n * (2 * NT + 1) + NT)
                    ins = dve.bn_aggr(moments[:, t, :], stats[:, t, :])
                    ins.then_inc(stat_step, 1)
                dve.wait_ge(stat_step, n * (2 * NT + 1) + 2 * NT)
                dve.sem_inc(var_ready, 1)

            def layer_norm(n, scale_col, bias_col, xn, ln_f):
                dve.wait_ge(std_ready, n + 1)
                dve.reciprocal(rstd[:, :], std[:, :]).then_inc(stat_step, 1)
                dve.wait_ge(stat_step, (n + 1) * (2 * NT + 1))
                for t in range(NT):
                    if t >= 2:
                        dve.wait_ge(xn_moved, n * NT + t - 1)
                    dve.tensor_scalar(xn[:, t % 2, :], x[:, t, :], moments[:, t, 0:1], rstd[:, t:t + 1],
                                      ALU.subtract, ALU.mult).then_inc(xn_ready, 1)
                for half in range(2):
                    for f in range(KT):
                        k = half * KT + f
                        dve.wait_ge(ln_hi_done, n * 2 * KT + k + 1)
                        if k >= 2:
                            dve.wait_ge(h_ready, n * 2 * KT + k - 1)
                        dve.tensor_scalar(ln_f[:, k % 2, :], ps[:, LN_BANK(half, f), :],
                                          mod_cols[:, scale_col, f:f + 1], mod_cols[:, bias_col, f:f + 1],
                                          ALU.mult, ALU.add).then_inc(ln_f_step, 1)
                        tok = slice(half * HALF, (half + 1) * HALF)
                        dve.wait_ge(ln_f_step, n * 2 * KT + k + 1)
                        dve.tensor_tensor(h_lo[:, f, tok], ln_f[:, k % 2, :], r32(h_hi[:, f, tok]),
                                          ALU.subtract).then_inc(h_ready, 1)

            statistics(0)
            dve.wait_ge(mod_done, 1)
            dve.tensor_scalar(mod_cols[:, 0, :], ps[:, 0, 0:KT], 1.0, None, ALU.add).then_inc(gate_step, 1)
            dve.tensor_copy(mod_cols[:, 1, :], ps[:, 0, KT:2 * KT]).then_inc(gate_step, 1)
            dve.tensor_scalar(mod_cols[:, 2, :], ps[:, 0, 2 * KT:3 * KT], 1.0, None, ALU.add).then_inc(gate_step, 1)
            dve.tensor_copy(mod_cols[:, 3, :], ps[:, 0, 3 * KT:4 * KT]).then_inc(gate_step, 1)
            for m, gate in enumerate((gate_a, gate_b)):
                at_start = 4 + 5 * m
                value, size = g_tmp[:, m, 0, :], g_tmp[:, m, 1, :]
                dve.tensor_copy(value, ps[:, 1 + m, :]).then_inc(gate_step, 1)
                dve.wait_ge(gate_step, at_start + 1)
                dve.scalar_tensor_tensor(out=size, in0=value, scalar=-1.0, in1=value, op0=ALU.mult, op1=ALU.max
                                         ).then_inc(gate_step, 1)
                dve.wait_ge(gate_step, at_start + 2)
                dve.tensor_scalar(size, size, 0.25, None, ALU.max).then_inc(gate_step, 1)
                dve.tensor_scalar(value, value, 0.0, 2.0, ALU.is_ge, ALU.mult).then_inc(gate_step, 1)
                dve.wait_ge(gate_step, at_start + 4)
                dve.scalar_tensor_tensor(out=gate[:, :], in0=value, scalar=-1.0, in1=size, op0=ALU.add,
                                         op1=ALU.mult).then_inc(gate_step, 1)
            dve.wait_ge(gate_step, 14)
            dve.sem_inc(mod_ready, 2)
            layer_norm(0, 0, 1, xn, ln_f)

            dve.wait_ge(consts_loaded, 48)
            with dve.Fori(0, PAIRS) as it:
                def project_lo(kind, hd, n, half):
                    G_i = group_index(kind, hd, n, half)
                    dve.wait_ge(proj_hi, it * NG + (G_i + 1))
                    bank = ps[:, G_i % 4 if G_i < len(HEAD_GROUPS) else M_BANK, :]
                    tok = slice(half * HALF, (half + 1) * HALF)
                    if kind == "q":
                        ins = dve.scalar_tensor_tensor(out=q_lo[:, n, tok], in0=bank,
                                                       scalar=consts[:, 0, hd, n:n + 1],
                                                       in1=r32(q_hi[:, n, tok]), op0=ALU.mult, op1=ALU.subtract)
                    elif kind == "k":
                        ins = dve.tensor_tensor(k_lo[:, tok], bank, r32(k_hi[:, tok]), ALU.subtract)
                    else:
                        ins = dve.tensor_tensor(v_lo[:, :, n, :],
                                                bank[:, 0:2 * D].rearrange("p (a d) -> p a d", a=2),
                                                r32(v_hi[:, :, n, :]), ALU.subtract)
                    ins.then_inc(proj_split, 1)

                def bias_and_minimum(hd, i, g, blocks_before):
                    n = (hd * NT + i) * G + g
                    dve.wait_ge(s_done, it * (UNITS * G) + (n + 1))
                    dve.wait_ge(t_done, it * BLOCKS + (blocks_before + 1))
                    alone(dve)
                    w = (i + 1) * P
                    bank = 2 * (g % 2)
                    dve.tensor_tensor_reduce(
                        out=probs[:, i % 2, g, 0:w],
                        in0=ps[:, bank:bank + 2, :].rearrange("p b n -> p (b n)")[:, 0:w],
                        in1=sdist[:, S - w:S], scale=1.0, scalar=3.0e38, op0=ALU.add, op1=ALU.min,
                        accum_out=low[:, i % 2, g:g + 1]).then_inc(s_biased, 1)
                    dve.wait_ge(s_biased, it * (UNITS * G) + (n + 3))
                    dve.tensor_tensor(shift[:, i % 2, g:g + 1], low[:, i % 2, g:g + 1],
                                      consts[:, 1, hd, g:g + 1], ALU.mult).then_inc(shift_ready, 1)

                def invert(hd, i, g):
                    dve.wait_ge(exp_done, it * (UNITS * G) + ((hd * NT + i) * G + g + 1))
                    dve.reciprocal(inv[:, i % 2, g:g + 1], rowsum[:, i % 2, g:g + 1]).then_inc(inv_ready, 1)

                def add_product(n):
                    i = n % NT
                    dve.wait_ge(y_done, it * UNITS + (n + 2))
                    dve.tensor_tensor(x[:, i, :], ps[:, M_BANK, :], x[:, i, :], ALU.add).then_inc(x_added, 1)

                dve.tensor_copy(consts[:, :, :, :], table[:, bass.ds(it, 1), :, :, :].rearrange(
                    "p a c h g -> p (a c) h g")).then_inc(head_consts, 1)
                dve.wait_ge(head_consts, it + 1)
                for grp in HEAD_GROUPS:
                    project_lo(*grp)
                for g in range(G):
                    bias_and_minimum(A, 0, g, 0)
                for g in range(G):
                    invert(A, 0, g)
                for hd in range(2):
                    for i in range(NT):
                        nxt = next_unit(hd, i)
                        waiting, exps = [], []
                        for s in range(i + 2):
                            if s <= i:
                                b = block_index(hd, i, s)
                                dve.wait_ge(pt_hi_done, it * BLOCKS + (b + 1))
                                dve.tensor_tensor(pt_lo[:, b % 2, :], ps[:, T_BANK + b % 2, :],
                                                  r32(pt_hi[:, b % 2, :]), ALU.subtract).then_inc(pt_split, 1)
                            for slot, grp, _u in FILL.get((hd, i), []):
                                if slot == s:
                                    project_lo(*grp)
                            if nxt:
                                fresh = [g for g in range(G) if score_slots(hd, i)[g] == s]
                                for g in fresh:
                                    bias_and_minimum(*nxt, g, block_index(hd, i, 0))
                                for g in waiting:
                                    invert(*nxt, g)
                                waiting = fresh
                            if s == wo_slot(hd, i) and i > 0:
                                add_product(hd * NT + i - 1)
                            elif s == wo_slot(hd, i) and hd == B:
                                add_product(NT - 1)
                        for g in waiting:
                            invert(*nxt, g)
                        if i == 0:
                            for g in range(G):
                                dve.wait_ge(wo_hi_done, it * (2 * G) + (hd * G + g + 1))
                                ins = dve.tensor_tensor(wo_lo[:, g, :], wo_raw[:, g, :], r32(wo_hi[:, g, :]),
                                                        ALU.subtract)
                                ins.then_inc(wo_ready, 1)
                        n = hd * NT + i
                        dve.wait_ge(o_hi_done, it * UNITS + (n + 1))
                        dve.tensor_tensor(o_lo[:, :], ps[:, O_BANK, :], r32(o_hi[:, :]), ALU.subtract
                                          ).then_inc(o_split, 1)
                add_product(UNITS - 1)

            dve.wait_ge(x_added, PAIRS * UNITS + 1)
            statistics(1)
            layer_norm(1, 2, 3, xn2, ln_f2)

            dve.wait_ge(shifts_loaded, 16)
            steps = [0]

            def dequantise(n, q, z, s, w, groups, rows, loaded, count, buffer_free):
                width = q.shape[-1]
                k = n_dq[0]
                n_dq[0] += 1
                dve.wait_ge(loaded, count)
                size = groups * width
                nv = nib[0:rows, 0:size].rearrange("p (k n) -> p k n", k=groups)
                zv = znib[0:rows, 0, 0:size]
                zm = znib[0:rows, 1, 0:size]
                dve.wait_ge(wf_ready, 4 + k)
                if buffer_free:
                    buffer_free()
                dve.tensor_scalar(nv, q, shifts[0:rows, 0:1], 15, ALU.logical_shift_right, ALU.bitwise_and
                                  ).then_inc(dq_step, 1)
                z4d = z.unsqueeze(3).to_broadcast([rows, groups, width // PACK, PACK])
                sh = shifts[0:rows, 1:1 + PACK].unsqueeze(1).unsqueeze(1).to_broadcast(
                    [rows, groups, width // PACK, PACK])
                dve.tensor_tensor(zv.rearrange("p (k a b) -> p k a b", k=groups, b=PACK), z4d, sh,
                                  ALU.logical_shift_right).then_inc(dq_step, 1)
                dve.wait_ge(dq_step, 4 * k + 2)
                dve.tensor_scalar(zm, zv, 15, None, ALU.bitwise_and).then_inc(dq_step, 1)
                dve.wait_ge(dq_step, 4 * k + 3)
                dve.tensor_tensor(dif[0:rows, 0:size], nib[0:rows, 0:size], zm, ALU.subtract).then_inc(dq_step, 1)
                dve.wait_ge(dq_step, 4 * k + 4)
                dve.scalar_tensor_tensor(out=w[0:rows, 0:size].rearrange("p (k n) -> p k n", k=groups),
                                         in0=dif[0:rows, 0:size].rearrange("p (k n) -> p k n", k=groups),
                                         scalar=-1.0, in1=s, op0=ALU.add, op1=ALU.mult).then_inc(wf_ready, 1)

            n_dq = [0]

            def dequantise_gu(c, par, width):
                for m in range(2):
                    n = 2 * c + m
                    dequantise(n, q4[:, par, m, :, 0:width], z4[:, par, m, :, 0:width // PACK],
                               s4[:, par, m, :, 0:width], wf[:, m, :], KT, P, gu_loaded[par],
                               (c // 2 + 1) * 16 * 2 * (KT + 2),
                               (lambda: dve.wait_ge(wf_split, n - 1)) if n >= 2 else None)

            def ffn_chunk(c, par, width, following):
                for half in range(2):
                    n = c * 2 + half
                    dve.wait_ge(sig_done, n + 1)
                    if n >= 1:
                        dve.wait_ge(act_ready, n)
                    dve.tensor_tensor(act1[0:width, :], ps[0:width, 2 * (n % 4), :], sig[0:width, :], ALU.mult
                                      ).then_inc(silu_done, 1)
                    dve.wait_ge(silu_done, n + 1)
                    dve.wait_ge(up_done, n + 1)
                    if n >= 2:
                        dve.wait_ge(act_split, n - 1)
                    dve.tensor_tensor(act2[0:width, half, :], ps[0:width, 2 * (n % 4) + 1, :],
                                      act1[0:width, :], ALU.mult).then_inc(act_ready, 1)

            dequantise_gu(0, 0, P)
            for c in range(NCH):
                width = P if c < NC_FULL else C_LAST
                if c + 1 < NCH:
                    dequantise_gu(c + 1, (c + 1) % 2, P if c + 1 < NC_FULL else C_LAST)
                ffn_chunk(c, c % 2, width, 0)
            for c in range(NCH):
                n = P if c < NC_FULL else C_LAST
                def free(c=c):
                    dve.wait_ge(wf_split, 2 * NCH + c - 1)
                dequantise(2 * NCH + c, qd[0:n, c % 2, :].unsqueeze(1), zd[0:n, c % 2, :].unsqueeze(1),
                           sd[0:n, c % 2, :].unsqueeze(1), wf[:, c % 2, :], 1, n, d_loaded[c % 2],
                           (c // 2 + 1) * 48, free)
            for t in range(NT):
                dve.wait_ge(o16_done, t + 1)
                if t >= 2:
                    dve.wait_ge(out_stored[t % 2], 16 * (t // 2))
                dve.tensor_tensor(fin[:, t % 2, :], o16[:, t % 2, :], gate_b[:, :], ALU.mult).then_inc(fin_step, 1)
                dve.wait_ge(fin_step, t + 1)
                dve.tensor_tensor(fin[:, t % 2, :], fin[:, t % 2, :], x[:, t, :], ALU.add).then_inc(fin_ready, 1)

        @block.tensor
        def _(pe):
            pe.sem_inc(proj_done, 1)
            pe.sem_inc(t_done, 1)
            pe.sem_inc(pv_done, 2)
            pe.sem_inc(y_done, 1)

            def products(out_ap, terms, done=None):
                for n, (l_hi, l_lo, r_hi, r_lo) in enumerate(terms):
                    pe.matmul(out_ap, l_hi, r_hi, start=(n == 0), stop=False)
                    pe.matmul(out_ap, l_hi, r_lo, start=False, stop=False)
                    ins = pe.matmul(out_ap, l_lo, r_hi, start=False, stop=(n == len(terms) - 1))
                return ins

            pe.wait_ge(silu_ready, 1)
            for j, m in enumerate((1, 0, 4, 3)):
                pe.wait_ge(mod_loaded[m], 16)
                for f in range(KT):
                    for k in range(KT):
                        pe.matmul(ps[:, 0, j * KT + f:j * KT + f + 1], wmod[:, m, k, f * P:(f + 1) * P],
                                  silu_c[:, k:k + 1], start=(k == 0), stop=(k == KT - 1))
            for j, m in enumerate((2, 5)):
                pe.wait_ge(mod_loaded[m], 16)
                for k in range(KT):
                    ins = pe.matmul(ps[:, 1 + j, :], silu_b[:, k, :], wmod[:, m, k, :],
                                    start=(k == 0), stop=(k == KT - 1))
            ins.then_inc(mod_done, 1)

            def layer_norm(n, xn):
                for t in range(NT):
                    pe.wait_ge(xn_ready, n * NT + t + 1)
                    for f in range(KT):
                        c = (t % 4) * P
                        ins = pe.transpose(ps[:, LN_BANK(t // 4, f), c:c + P], xn[:, t % 2, f * P:(f + 1) * P],
                                           ident[:, :])
                    ins.then_inc(xn_moved, 1)

            pe.wait_ge(consts_loaded, 48)
            pe.wait_ge(mod_ready, 2)
            layer_norm(0, xn)
            pe.wait_ge(h_ready, 2 * KT)

            with pe.Fori(0, PAIRS) as it:
                def project(kind, hd, n, half, use):
                    G_i = group_index(kind, hd, n, half)
                    in_head = G_i < len(HEAD_GROUPS)
                    if in_head and G_i < 4:
                        pe.wait_ge(s_biased, it * (UNITS * G) + (1 + G_i // 2))
                    elif in_head:
                        pe.wait_ge(proj_split, it * NG + (G_i - 4 + 2))
                    else:
                        pe.wait_ge(proj_split, it * NG + (G_i + 1))
                    bank = ps[:, G_i % 4 if in_head else M_BANK, :]
                    tok = slice(half * HALF, (half + 1) * HALF)
                    slot = use % RING
                    if kind == "v":
                        pe.wait_ge(w_ready, it * NU + (use + 2 + RING))
                        tt = slice(n * P, (n + 1) * P)
                        ins = products(bank[:, 0:2 * D],
                                       [(h_hi[:, k, tt], h_lo[:, k, tt], w_hi[:, slot:slot + 2, k, :],
                                         w_lo[:, slot:slot + 2, k, :]) for k in range(KT)])
                    else:
                        pe.wait_ge(w_ready, it * NU + (use + 1 + RING))
                        ins = products(bank, [(w_hi[:, slot, k, :], w_lo[:, slot, k, :], h_hi[:, k, tok],
                                               h_lo[:, k, tok]) for k in range(KT)])
                    ins.then_inc(proj_done, 1)

                def score(hd, i, g):
                    n = (hd * NT + i) * G + g
                    half = i // 4
                    need = max(group_index("q", hd, g, half), group_index("k", hd, 0, 1))
                    if n == 0 or n == 1:
                        need = len(HEAD_GROUPS) - 1
                    pe.wait_ge(proj_split, it * NG + (need + 2))
                    pe.wait_ge(s_biased, it * (UNITS * G) + (n + 1))
                    lo = slice(i * P, (i + 1) * P)
                    for b, width in enumerate(score_banks(i)):
                        keys = slice(b * 512, b * 512 + width)
                        ins = products(ps[:, 2 * (g % 2) + b, 0:width],
                                       [(q_hi[:, g, lo], q_lo[:, g, lo], k_hi[:, keys], k_lo[:, keys])])
                    ins.then_inc(s_done, 1)

                def transpose_block(hd, i, s):
                    b = block_index(hd, i, s)
                    pe.wait_ge(pt_split, it * BLOCKS + (b + 1))
                    for g in range(G):
                        if s == 0:
                            pe.wait_ge(normed, it * (UNITS * G) + ((hd * NT + i) * G + g + 1))
                        ins = pe.transpose(ps[:, T_BANK + b % 2, g * P:(g + 1) * P],
                                           probs[:, i % 2, g, s * P:(s + 1) * P], ident[:, :])
                    ins.then_inc(t_done, 1)

                def attend(hd, i, s):
                    b = block_index(hd, i, s)
                    pe.wait_ge(pt_split, it * BLOCKS + (b + 3))
                    if s == 0:
                        pe.wait_ge(o_split, it * UNITS + (hd * NT + i + 1))
                    o, v1, v2 = ps[:, O_BANK, :], v_hi[:, hd, s, :], v_lo[:, hd, s, :]
                    p1, p2 = pt_hi[:, b % 2, :], pt_lo[:, b % 2, :]
                    pe.matmul(o, v1, p1, start=(s == 0), stop=False)
                    pe.matmul(o, v1, p2, start=False, stop=False)
                    ins = pe.matmul(o, v2, p1, start=False, stop=(s == i))
                    ins.then_inc(pv_done, 1)
                    return ins

                def output_product(n, groups_before):
                    pe.wait_ge(o_split, it * UNITS + (n + 2))
                    pe.wait_ge(wo_ready, it * (2 * G) + ((n // NT + 1) * G + 1))
                    pe.wait_ge(x_added, it * UNITS + (n + 1))
                    pe.wait_ge(proj_split, it * NG + (groups_before + 1))
                    cols = [slice(g * P, (g + 1) * P) for g in range(G)]
                    products(ps[:, M_BANK, :], [(o_hi[:, cols[g]], o_lo[:, cols[g]], wo_hi[:, g, :], wo_lo[:, g, :])
                                                for g in range(G)]).then_inc(y_done, 1)

                done = 0
                u_of = [0, 0] + [1] * NT + [3, 4, 5, 6]
                for j, grp in enumerate(HEAD_GROUPS):
                    project(*grp, u_of[j])
                    done += 1
                for g in range(G):
                    score(A, 0, g)
                for hd in range(2):
                    for i in range(NT):
                        n = hd * NT + i
                        nxt = next_unit(hd, i)
                        for s in range(i + 2):
                            if s <= i:
                                transpose_block(hd, i, s)
                            for slot, grp, use in FILL.get((hd, i), []):
                                if slot == s:
                                    pe.wait_ge(x_added, it * UNITS + max(n, 1))
                                    project(*grp, use)
                                    done += 1
                            if nxt:
                                for g in range(G):
                                    if score_slots(hd, i)[g] == s:
                                        score(*nxt, g)
                            if s == wo_slot(hd, i) and n > 0:
                                output_product(n - 1, done)
                            if s >= 1:
                                attend(hd, i, s - 1)
                output_product(UNITS - 1, done)

            pe.wait_ge(x_added, PAIRS * UNITS + 1)
            layer_norm(1, xn2)
            pe.wait_ge(h_ready, 4 * KT)

            for c in range(NCH):
                width, par = (P if c < NC_FULL else C_LAST), c % 2
                pe.wait_ge(wf_split, 2 * c + 2)
                for half in range(2):
                    n = 2 * c + half
                    tok = slice(half * HALF, (half + 1) * HALF)
                    if n >= 4:
                        pe.wait_ge(act_ready, n - 3)
                    for m, done in ((0, gate_done), (1, up_done)):
                        products(ps[0:width, 2 * (n % 4) + m, :],
                                 [(gu_hi[:, par, m, k, 0:width], gu_lo[:, par, m, k, 0:width],
                                   h_hi[:, k, tok], h_lo[:, k, tok]) for k in range(KT)]).then_inc(done, 1)
            pe.wait_ge(act_ready, 2 * NCH)
            pe.wait_ge(act_split, 2 * NCH)
            for c in range(NCH):
                rows, par = (P if c < NC_FULL else C_LAST), c % 2
                pe.wait_ge(wf_split, 2 * NCH + c + 1)
                for t in range(NT):
                    tok = slice(t * P, (t + 1) * P)
                    l1, l2, r1, r2 = t_hi[0:rows, c, tok], t_lo[0:rows, c, tok], d_hi[0:rows, par, :], d_lo[0:rows, par, :]
                    pe.matmul(ps[:, t, :], l1, r1, start=(c == 0), stop=False)
                    pe.matmul(ps[:, t, :], l1, r2, start=False, stop=False)
                    ins = pe.matmul(ps[:, t, :], l2, r1, start=False, stop=(c == NCH - 1))
                    if c == NCH - 1:
                        ins.then_inc(y2_done, 1)
                if c < NCH - 1:
                    ins.then_inc(d_used, 1)


def kernel(**inputs):
    import numpy as _np
    import concourse.bacc as _bacc
    from concourse import mybir as _mybir
    from concourse.bass_utils import run_bass_kernel_spmd as _run

    nc = _bacc.Bacc("TRN2", target_bir_lowering=False, num_devices=1)
    arrays = {}

    def dram(name, a):
        a = _np.ascontiguousarray(a)
        arrays[name] = a
        return nc.dram_tensor(name, a.shape, _mybir.dt.from_np(a.dtype), kind="ExternalInput").ap()

    p = _np.arange(P)[:, None]
    rel = p + (S - P) - _np.arange(S)[None, :]
    sqrt_dist = _np.where(rel >= 0, _np.sqrt(_np.maximum(rel, 0).astype(_np.float32)),
                          _np.float32(MASKED)).astype(_np.float32)
    slope_base = 2.0 ** (-8.0 / NH)
    slopes = (slope_base ** _np.arange(1, NH + 1, dtype=_np.float32)).astype(_np.float32)
    per_head = slopes.reshape(PAIRS, 1, 2, G)
    table = _np.concatenate([-_np.float32(D ** -0.5) / per_head, per_head, -per_head], axis=1)
    table = _np.broadcast_to(table[None], (P,) + table.shape).astype(_np.float32)
    shifts = _np.concatenate([_np.broadcast_to(4 * (p % PACK), (P, 1)),
                              _np.broadcast_to(4 * _np.arange(PACK), (P, PACK))], axis=1).astype(_np.int32)

    args = [
        dram("x_dram", inputs["L0_attn_hidden_states"][0]),
        dram("w_qkv_dram", inputs["L0_attn_w_qkv"]),
        dram("w_o_dram", inputs["L0_attn_w_o"]),
        [dram(f"{m}_q_dram", inputs[f"L0_ffn_{m}_qweight"]) for m in ("gate", "up", "down")],
        [dram(f"{m}_s_dram", inputs[f"L0_ffn_{m}_scales"]) for m in ("gate", "up", "down")],
        [dram(f"{m}_z_dram", inputs[f"L0_ffn_{m}_zeros"]) for m in ("gate", "up", "down")],
        dram("c_dram", _np.asarray(inputs["L0_c"]).reshape(KT, P).T),
        dram("w_mod_dram", inputs["L0_wmod"]),
        dram("sqrt_dist_dram", sqrt_dist),
        dram("head_table_dram", table),
        dram("ident_dram", _np.eye(P, dtype=_np.float32)),
        dram("shifts_dram", shifts),
        nc.dram_tensor("out_dram", (S, H), F32, kind="ExternalOutput").ap(),
    ]
    build(nc, *args)
    r = _run(nc, [arrays], core_ids=[0])
    return r.results[0]["out_dram"].reshape(1, S, H)
```

```python
import numpy as np
import concourse.bass as bass
from concourse import mybir

F32 = mybir.dt.float32
F32R = mybir.dt.float32r
F16 = mybir.dt.float16
I32 = mybir.dt.int32
ALU = mybir.AluOpType
ACT = mybir.ActivationFunctionType

P = 128
S = 1024
H = 512
NH, NKV, D = 32, 8, 128
G = NH // NKV
NT = S // P
KT = H // P
HALF = 512
INTER = 1376
PACK = 8
NC_FULL, C_LAST = INTER // P, INTER % P
NCH = NC_FULL + 1
ROWS = P // PACK
MASKED = 1.0e30
EPS = 1e-5

PAIRS = NKV // 2
UNITS = 2 * NT
BLOCKS = NT * (NT + 1)

A, B = 0, 1
USES = ([("k", A, 0), ("v", A, 0), ("v", B, 0)] + [("q", A, g) for g in range(G)]
        + [("q", A, g) for g in range(G)] + [("q", B, g) for g in range(G)] + [("k", B, 0)]
        + [("q", B, g) for g in range(G)])
NU = len(USES)
RING = 4
LAG = 2
LNF = 4
PT = 3
USE_QA1, USE_QB0, USE_KB, USE_QB1 = 7, 11, 15, 16
HEAD_GROUPS = ([("k", A, 0, h) for h in range(2)] + [("v", A, t, 0) for t in range(NT)]
               + [("q", A, g, 0) for g in range(G)])
FILL = {}
for _i in range(G):
    FILL[(A, _i)] = [(0, ("q", A, _i, 1), USE_QA1 + _i)]
    FILL[(A, G + _i)] = [(0, ("q", B, _i, 0), USE_QB0 + _i)]
    FILL[(B, _i)] = [(0, ("q", B, _i, 1), USE_QB1 + _i)]
FILL[(A, NT - 1)] += [(1, ("k", B, 0, 0), USE_KB), (2, ("k", B, 0, 1), USE_KB)]
GROUPS = HEAD_GROUPS + [f[1] for hd in range(2) for i in range(NT) for f in FILL.get((hd, i), [])]
NG = len(GROUPS)


LAST_GROUP = []
for _u, (_k, _hd, _g) in enumerate(USES):
    _of = [n for n, (k, hd, m, half) in enumerate(GROUPS)
           if k == _k and (k == "v" or hd == _hd) and (k != "q" or m == _g)]
    if _k == "q":
        _of = [_of[0 if _u in range(3, USE_QA1) or _u in range(USE_QB0, USE_KB) else 1]]
    LAST_GROUP.append(max(_of))


def group_index(kind, hd, n, half):
    return GROUPS.index((kind, hd, n, half))


def block_index(hd, i, s):
    return hd * (BLOCKS // 2) + i * (i + 1) // 2 + s


def score_slots(hd, i):
    if hd == A and i == NT - 1:
        return [3, 4, 5, 6]
    return {0: [0, 0, 1, 1], 1: [0, 0, 1, 2], 4: [0, 1, 3, 4], 5: [0, 1, 3, 4], 6: [0, 2, 3, 5]}.get(i, [0, 1, 2, 3])


def wo_slot(hd, i):
    return i + 1


def slots(i):
    return range(i + 1 + LAG)


def uses_of(unit):
    return sorted({f[2] for f in FILL.get(unit, [])}) if unit else []


def next_unit(hd, i):
    if i + 1 < NT:
        return hd, i + 1
    return (B, 0) if hd == A else None


def score_banks(i):
    n = (i + 1) * P
    return [max(256, min(n, 512))] + ([max(256, n - 512)] if n > 512 else [])


def build(nc, x_in, w_qkv, w_o, qw, sc, zr, c_in, w_mod, sqrt_dist, head_table, ident_in, shift_in, out):
    at = [((nc.sbuf_base if not callable(nc.sbuf_base) else nc.sbuf_base()) + 63) // 64 * 64]

    def place(name, shape, dtype, offset=None):
        size = int(np.prod(shape[1:])) * mybir.dt.size(dtype)
        where = at[0] if offset is None else offset
        if offset is None:
            at[0] += (size + 31) // 32 * 32
        return nc.alloc_sbuf_tensor_at(name, shape, dtype, offset=where)

    x = place("x", [P, NT, H], F32)
    h_hi = place("h_hi", [P, KT, S], F32R)
    h_lo = place("h_lo", [P, KT, S], F32R)
    ident = place("ident", [P, P], F32)
    mod_cols = place("mod_cols", [P, 4, KT], F32)
    stats = place("stats", [P, NT, 6], F32)
    moments = place("moments", [P, NT, 2], F32)
    std = place("std", [P, NT], F32)
    rstd = place("rstd", [P, NT], F32)
    eps_col = place("eps_col", [P, 1], F32)
    silu_c = place("silu_c", [P, KT], F32)
    base = at[0]

    q_hi = place("q_hi", [P, G, S], F32R)
    q_lo = place("q_lo", [P, G, S], F32R)
    k_hi = place("k_hi", [P, S], F32R)
    k_lo = place("k_lo", [P, S], F32R)
    v_hi = place("v_hi", [P, 2, NT, D], F32R)
    v_lo = place("v_lo", [P, 2, NT, D], F32R)
    probs = place("probs", [P, 2, G, S], F32)
    pt_hi = place("pt_hi", [P, PT, G * P], F32R)
    pt_lo = place("pt_lo", [P, PT, G * P], F32R)
    o_hi = place("o_hi", [P, G * P], F32R)
    o_lo = place("o_lo", [P, G * P], F32R)
    ring_at = at[0]
    w_raw = place("w_raw", [P, RING, KT, P], F32)
    w_hi = place("w_hi", [P, RING, KT, P], F32R)
    w_lo = place("w_lo", [P, RING, KT, P], F32R)
    wo_raw_at = at[0]
    wo_raw = place("wo_raw", [P, G, H], F32)
    wo_hi = place("wo_hi", [P, G, H], F32R)
    wo_lo = place("wo_lo", [P, G, H], F32R)
    sdist = place("sdist", [P, S], F32)
    gate_a = place("gate_a", [P, H], F32)
    table = place("table", [P, PAIRS, 3, 2, G], F32)
    consts = place("consts", [P, 3, 2, G], F32)
    low = place("low", [P, 2, G], F32)
    shift = place("shift", [P, 2, G], F32)
    rowsum = place("rowsum", [P, 2, G], F32)
    inv = place("inv", [P, 2, G], F32)
    assert at[0] <= (nc.sbuf_usable_end() if callable(nc.sbuf_usable_end) else nc.sbuf_usable_end), at[0]

    at[0] = base
    wmod = place("wmod", [P, 3, KT, H], F32)
    xn = place("xn", [P, 2, H], F32)
    ln_f = place("ln_f", [P, LNF, HALF], F32)
    c_col = place("c_col", [P, KT], F32)
    c_tmp = place("c_tmp", [P, 3, KT], F32)
    silu_b = place("silu_b", [P, KT, P], F32)
    g_tmp = place("g_tmp", [P, 2, H], F32)

    at[0] = base
    wmod2 = place("wmod2", [P, 3, KT, H], F32, base)
    silu_b2 = place("silu_b2", [P, KT, P], F32, base + 3 * KT * H * 4)
    t_hi = place("t_hi", [P, NCH, S], F32R)
    t_lo = place("t_lo", [P, NCH, S], F32R)
    ln_f2_at = at[0] - LNF * HALF * 4
    ln_f2 = place("ln_f2", [P, LNF, HALF], F32, ln_f2_at)
    xn2 = place("xn2", [P, 2, H], F32, ln_f2_at - 2 * H * 4)
    gu_hi = place("gu_hi", [P, 2, 2, KT, P], F32R)
    gu_lo = place("gu_lo", [P, 2, 2, KT, P], F32R)
    assert at[0] <= ring_at
    at[0] = ring_at
    s4 = place("s4", [P, 2, 2, KT, P], F16)
    z4 = place("z4", [P, 2, 2, KT, P // PACK], I32)
    nib = place("nib", [P, KT * P], I32)
    znib = place("znib", [P, 2, KT * P], I32)
    dif = place("dif", [P, KT * P], F32)
    wf = place("wf", [P, 2, KT * P], F32)
    shifts = place("shifts", [P, 1 + PACK], I32)
    sig = place("sig", [P, HALF], F32)
    act1 = place("act1", [P, HALF], F32)
    o16 = place("o16", [P, 2, H], F16)
    assert at[0] <= wo_raw_at
    at[0] = wo_raw_at
    q4 = place("q4", [P, 2, 2, KT, P], I32)
    act2_at = at[0]
    act2 = place("act2", [P, 2, HALF], F32)
    qd = place("qd", [P, 2, H], I32)
    sd = place("sd", [P, 2, H], F16)
    zd = place("zd", [P, 2, H // PACK], I32)
    d_hi = place("d_hi", [P, 2, H], F32R)
    d_lo = place("d_lo", [P, 2, H], F32R)
    gate_b = place("gate_b", [P, H], F32)
    gate_size = place("gate_size", [P, H], F32)
    fin = place("fin", [P, 2, H], F32, act2_at)
    assert at[0] <= (nc.sbuf_usable_end() if callable(nc.sbuf_usable_end) else nc.sbuf_usable_end), at[0]

    ps = nc.alloc_psum_tensor("ps", [P, 8, 512], F32)
    GATE_BANK = 3
    T_BANK, O_BANK, M_BANK = 4, 6, 7

    def r32(ap):
        return ap.bitcast(F32)

    sem = lambda name: nc.alloc_semaphore(name)
    waits_passed = sem("waits_passed")
    x_in_sem = [sem(f"x_loaded{t}") for t in range(NT)]
    c_loaded = sem("c_loaded")
    consts_loaded = sem("consts_loaded")
    mod_loaded = [sem(f"mod_loaded{m}") for m in range(6)]
    silu_step = sem("silu_step")
    silu_exp = sem("silu_exp")
    silu_ready = sem("silu_ready")
    mod_done = sem("mod_done")
    cols_ready = sem("cols_ready")
    gate_a_ready = sem("gate_a_ready")
    gate_row = sem("gate_row")
    gate_step = sem("gate_step")
    stat_step = sem("stat_step")
    var_ready = sem("var_ready")
    std_ready = sem("std_ready")
    xn_ready = sem("xn_ready")
    xn_moved = sem("xn_moved")
    ln_f_done = sem("ln_f_done")
    h_hi_done = sem("h_hi_done")
    h_lo_dve = sem("h_lo_dve")
    h_lo_pool = sem("h_lo_pool")
    w_loaded = [sem(f"w_loaded{i}") for i in range(RING)]
    w_hi_done = sem("w_hi_done")
    w_ready = sem("w_ready")
    wo_loaded = sem("wo_loaded")
    wo_scaled = sem("wo_scaled")
    wo_hi_done = sem("wo_hi_done")
    wo_ready = sem("wo_ready")
    head_consts = sem("head_consts")
    proj_done = sem("proj_done")
    proj_hi = sem("proj_hi")
    proj_split = sem("proj_split")
    s_done = sem("s_done")
    s_biased = sem("s_biased")
    shift_ready = sem("shift_ready")
    exp_done = sem("exp_done")
    inv_ready = sem("inv_ready")
    normed = sem("normed")
    t_done = sem("t_done")
    pt_hi_done = sem("pt_hi_done")
    pt_split = sem("pt_split")
    pv_done = sem("pv_done")
    o_hi_done = sem("o_hi_done")
    o_split = sem("o_split")
    y_done = sem("y_done")
    x_added = sem("x_added")
    shifts_loaded = sem("shifts_loaded")
    gu_loaded = [sem(f"gu_loaded{i}") for i in range(2)]
    dq_step = sem("dq_step")
    wf_ready = sem("wf_ready")
    wf_hi = sem("wf_hi")
    wf_split = sem("wf_split")
    gate_done = sem("gate_done")
    up_done = sem("up_done")
    sig_done = sem("sig_done")
    silu_done = sem("silu_done")
    act_ready = sem("act_ready")
    act_hi = sem("act_hi")
    act_split = sem("act_split")
    d_loaded = [sem(f"d_loaded{i}") for i in range(2)]
    d_used = sem("d_used")
    y2_done = sem("y2_done")
    o16_done = sem("o16_done")
    fin_step = sem("fin_step")
    fin_ready = sem("fin_ready")
    out_stored = [sem(f"out_stored{i}") for i in range(2)]

    def alone(eng):
        eng.sem_inc(waits_passed, 1)

    W3 = w_qkv.rearrange("(k p) n -> p k n", p=P)

    def use_columns(u, it):
        kind, hd, g = USES[u]
        if kind == "q":
            return it * (2 * G * D) + (hd * G + g) * D
        return it * (2 * D) + (NH * D + (NKV * D if kind == "v" else 0) + hd * D)

    def h_lo_done(n, k):
        return (h_lo_pool if k % 2 else h_lo_dve), n * KT + k // 2 + 1

    LN_BANK = lambda half, f: half * KT + f

    block = nc.Block()
    with block:

        @block.sync
        def _(sp):
            for t in range(NT):
                sp.dma_start(x[:, t, :], x_in[t * P:(t + 1) * P, :]).then_inc(x_in_sem[t], 16)
            sp.dma_start(ident[:, :], ident_in).then_inc(consts_loaded, 16)
            wm = w_mod.rearrange("(k p) (m n) -> p m k n", p=P, m=6)
            sp.dma_start(table[:, :, :, :, :], head_table).then_inc(consts_loaded, 16)
            sp.dma_start(sdist[:, :], sqrt_dist).then_inc(consts_loaded, 16)
            with sp.Fori(0, PAIRS) as it:
                def load_wo(hd):
                    sp.wait_ge(wo_ready, (it * 2 + hd) * G + 1)
                    alone(sp)
                    rows = bass.ds(it * (2 * G * D) + hd * G * D, G * D)
                    sp.dma_start(wo_raw[:, :, :], w_o[rows, :].rearrange("(g p) n -> p g n", p=P)
                                 ).then_inc(wo_loaded, 16)

                for u in range(NU):
                    slot = u % RING
                    sp.wait_ge(w_ready, it * NU + (u + 1))
                    alone(sp)
                    sp.dma_start(w_raw[:, slot, :, :], W3[:, :, bass.ds(use_columns(u, it), P)]
                                 ).then_inc(w_loaded[slot], 16)
                    if u == 2:
                        load_wo(A)
                    if u == USE_QA1 + G:
                        load_wo(B)
            sp.wait_ge(s_done, PAIRS * UNITS * G)
            for j, m in enumerate((4, 3, 5)):
                sp.dma_start(wmod2[:, j, :, :], wm[:, m, :, :]).then_inc(mod_loaded[m], 16)
            sp.wait_ge(proj_done, PAIRS * NG + 1)
            sp.wait_ge(wo_ready, PAIRS * 2 * G + 1)
            sp.dma_start(shifts[:, :], shift_in).then_inc(shifts_loaded, 16)

            def load_gu(c, par, width, count):
                sp.wait_ge(wf_ready, count)
                alone(sp)
                for m in range(2):
                    cols = bass.ds(c * P, width)
                    for k in range(KT):
                        src = qw[m][k * ROWS:(k + 1) * ROWS, cols]
                        sp.dma_start(q4[:, par, m, k, 0:width],
                                     src.unsqueeze(1).to_broadcast([ROWS, PACK, width])
                                     ).then_inc(gu_loaded[par], 16)
                    sp.dma_start(s4[:, par, m, :, 0:width],
                                 sc[m][:, cols].unsqueeze(0).to_broadcast([P, KT, width])
                                 ).then_inc(gu_loaded[par], 16)
                    sp.dma_start(z4[:, par, m, :, 0:width // PACK],
                                 zr[m][:, bass.ds(c * (P // PACK), width // PACK)].unsqueeze(0)
                                 .to_broadcast([P, KT, width // PACK])).then_inc(gu_loaded[par], 16)

            with sp.Fori(0, NC_FULL // 2) as it:
                for par in range(2):
                    load_gu(it * 2 + par, par, P, it * 4 + (2 * par + 2))
            load_gu(NC_FULL, 0, C_LAST, 2 * NC_FULL + 2)

            def load_down(c):
                par, rows = c % 2, (ROWS if c < NC_FULL else C_LAST // PACK)
                sp.dma_start(qd[0:rows * PACK, par, :],
                             qw[2][c * ROWS:c * ROWS + rows, :].unsqueeze(1).to_broadcast([rows, PACK, H])
                             ).then_inc(d_loaded[par], 16)
                sp.dma_start(sd[:, par, :], sc[2][c:c + 1, :].to_broadcast([P, H])
                             ).then_inc(d_loaded[par], 16)
                sp.dma_start(zd[:, par, :], zr[2][c:c + 1, :].to_broadcast([P, H // PACK])
                             ).then_inc(d_loaded[par], 16)

            sp.wait_ge(x_added, PAIRS * UNITS + 1)
            for c in range(NCH):
                if c >= 2:
                    sp.wait_ge(wf_ready, 4 + 2 * NCH + (c - 1))
                load_down(c)
            for t in range(NT):
                sp.wait_ge(fin_ready, t + 1)
                sp.dma_start(out[t * P:(t + 1) * P, :], fin[:, t % 2, :]).then_inc(out_stored[t % 2], 16)
            for i in range(2):
                sp.wait_ge(out_stored[i], 16 * (NT // 2))

        @block.gpsimd
        def _(pool):
            pool.sem_inc(w_ready, RING)

            def layer_norm(n, ln_f):
                for k in range(1, 2 * KT, 2):
                    tok, f = slice(k // KT * HALF, (k // KT + 1) * HALF), k % KT
                    pool.wait_ge(h_hi_done, n * 2 * KT + k + 1)
                    pool.tensor_tensor(h_lo[:, f, tok], ln_f[:, k % LNF, :], r32(h_hi[:, f, tok]),
                                       ALU.subtract).then_inc(h_lo_pool, 1)

            layer_norm(0, ln_f)

            with pool.Fori(0, PAIRS) as it:
                def scale_wo(hd, g):
                    pool.wait_ge(wo_loaded, it * 32 + (hd + 1) * 16)
                    pool.tensor_tensor(wo_raw[:, g, :], wo_raw[:, g, :], gate_a[:, :], ALU.mult
                                       ).then_inc(wo_scaled, 1)

                def split_use(u):
                    slot = u % RING
                    pool.wait_ge(w_loaded[slot], it * (NU // RING * 16) + (u // RING + 1) * 16)
                    pool.wait_ge(proj_done, it * NG + (LAST_GROUP[u - RING] + 2 if u >= RING else 1))
                    alone(pool)
                    pool.tensor_scalar(w_hi[:, slot, :, :], w_raw[:, slot, :, :], 1.0, 1.0, ALU.mult, ALU.mult
                                       ).then_inc(w_hi_done, 1)
                    pool.wait_ge(w_hi_done, it * NU + (u + 1))
                    pool.tensor_tensor(w_lo[:, slot, :, :], w_raw[:, slot, :, :], r32(w_hi[:, slot, :, :]),
                                       ALU.subtract).then_inc(w_ready, 1)

                def normalise(hd, i, g):
                    pool.wait_ge(inv_ready, it * (UNITS * G) + ((hd * NT + i) * G + g + 1))
                    alone(pool)
                    rows = probs[:, i % 2, g, 0:(i + 1) * P]
                    pool.tensor_scalar(rows, rows, inv[:, i % 2, g:g + 1], 1.0, ALU.mult, ALU.mult
                                       ).then_inc(normed, 1)

                for u in range(RING):
                    split_use(u)
                pool.wait_ge(gate_a_ready, 1)
                for g in range(G):
                    scale_wo(A, g)
                for u in range(RING, USE_QA1 + 2):
                    split_use(u)
                for g in range(G):
                    normalise(A, 0, g)
                for hd in range(2):
                    for i in range(NT):
                        nxt = next_unit(hd, i)
                        if nxt:
                            for g in range(G):
                                normalise(*nxt, g)
                            for u in uses_of(next_unit(*nxt)):
                                split_use(u)
                        if hd == A and i >= G:
                            scale_wo(B, i - G)

            layer_norm(1, ln_f2)

            def lo_weights(n, m, par, width):
                pool.wait_ge(wf_hi, n + 1)
                pool.tensor_tensor(gu_lo[:, par, m, :, 0:width],
                                   wf[:, m, 0:KT * width].rearrange("p (k n) -> p k n", k=KT),
                                   r32(gu_hi[:, par, m, :, 0:width]), ALU.subtract).then_inc(wf_split, 1)

            def lo_activation(n, c, half, width):
                pool.wait_ge(act_hi, n + 1)
                tok = slice(half * HALF, (half + 1) * HALF)
                pool.tensor_tensor(t_lo[0:width, c, tok], act2[0:width, half, :], r32(t_hi[0:width, c, tok]),
                                   ALU.subtract).then_inc(act_split, 1)

            def ffn_chunk(c, par, width, following):
                if following:
                    for m in range(2):
                        lo_weights((c + 1) * 2 + m, m, 1 - par, following)
                for half in range(2):
                    lo_activation(c * 2 + half, c, half, width)

            for m in range(2):
                lo_weights(m, m, 0, P)
            for c in range(NC_FULL):
                ffn_chunk(c, c % 2, P, P if c + 1 < NC_FULL else C_LAST)
            ffn_chunk(NC_FULL, 0, C_LAST, 0)
            for c in range(NCH):
                n = P if c < NC_FULL else C_LAST
                pool.wait_ge(wf_hi, 2 * NCH + c + 1)
                pool.tensor_tensor(d_lo[0:n, c % 2, :], wf[0:n, c % 2, :], r32(d_hi[0:n, c % 2, :]),
                                   ALU.subtract).then_inc(wf_split, 1)

        @block.scalar
        def _(act):
            act.dma_start(c_col[:, :], c_in).then_inc(c_loaded, 16)
            wm = w_mod.rearrange("(k p) (m n) -> p m k n", p=P, m=6)
            for j, m in enumerate((1, 0, 2)):
                act.dma_start(wmod[:, j, :, :], wm[:, m, :, :]).then_inc(mod_loaded[m], 16)
            act.wait_ge(c_loaded, 16)
            nc.scalar.activation(c_tmp[:, 0, :], c_col[:, :], ACT.Exp, scale=-1.0).then_inc(silu_exp, 1)

            def layer_norm(n, scale_col, bias_col, ln_f):
                act.wait_ge(var_ready, n + 1)
                nc.scalar.activation(std[:, :], moments[:, :, 1], ACT.Sqrt, bias=eps_col[:, 0:1]
                                     ).then_inc(std_ready, 1)
                act.wait_ge(cols_ready, n + 1)
                for k in range(2 * KT):
                    half, f = k // KT, k % KT
                    act.wait_ge(xn_moved, n * NT + (half + 1) * (NT // 2))
                    if k >= LNF:
                        act.wait_ge(*h_lo_done(n, k - LNF))
                    nc.scalar.activation(ln_f[:, k % LNF, :], ps[:, LN_BANK(half, f), :], ACT.Identity,
                                         scale=mod_cols[:, scale_col, f:f + 1],
                                         bias=mod_cols[:, bias_col, f:f + 1]).then_inc(ln_f_done, 1)

            layer_norm(0, 0, 1, ln_f)

            with act.Fori(0, PAIRS) as it:
                def project_hi(kind, hd, n, half):
                    G_i = group_index(kind, hd, n, half)
                    act.wait_ge(proj_done, it * NG + (G_i + 2))
                    bank = ps[:, G_i % 4 if G_i < len(HEAD_GROUPS) else M_BANK, :]
                    tok = slice(half * HALF, (half + 1) * HALF)
                    if kind == "q":
                        ins = nc.scalar.activation(q_hi[:, n, tok], bank, ACT.Copy,
                                                   scale=consts[:, 0, hd, n:n + 1])
                    elif kind == "k":
                        ins = nc.scalar.activation(k_hi[:, tok], bank, ACT.Copy)
                    else:
                        ins = nc.scalar.activation(v_hi[:, :, n, :],
                                                   bank[:, 0:2 * D].rearrange("p (a d) -> p a d", a=2), ACT.Copy)
                    ins.then_inc(proj_hi, 1)

                def exponential(hd, i, g):
                    n = (hd * NT + i) * G + g
                    act.wait_ge(shift_ready, it * (UNITS * G) + (n + 1))
                    rows = probs[:, i % 2, g, 0:(i + 1) * P]
                    nc.scalar.activation(rows, rows, ACT.Exp, scale=consts[:, 2, hd, g:g + 1],
                                         bias=shift[:, i % 2, g:g + 1],
                                         accum_out=rowsum[:, i % 2, g:g + 1]).then_inc(exp_done, 1)

                act.wait_ge(head_consts, it + 1)
                for grp in HEAD_GROUPS:
                    project_hi(*grp)
                for g in range(G):
                    exponential(A, 0, g)
                for hd in range(2):
                    for i in range(NT):
                        nxt = next_unit(hd, i)
                        waiting = []
                        for s in slots(i):
                            if s <= i:
                                b = block_index(hd, i, s)
                                act.wait_ge(t_done, it * BLOCKS + (b + 2))
                                act.wait_ge(pv_done, it * BLOCKS + (b + 1))
                                nc.scalar.activation(pt_hi[:, b % PT, :], ps[:, T_BANK + b % 2, :], ACT.Copy
                                                     ).then_inc(pt_hi_done, 1)
                            for g in waiting:
                                exponential(*nxt, g)
                            waiting = []
                            for slot, grp, _u in FILL.get((hd, i), []):
                                if slot == s:
                                    project_hi(*grp)
                            if nxt:
                                waiting = [g for g in range(G) if score_slots(hd, i)[g] == s]
                        for g in waiting:
                            exponential(*nxt, g)
                        if i == 0:
                            act.wait_ge(y_done, it * UNITS + hd * NT + 1)
                            for g in range(G):
                                act.wait_ge(wo_scaled, it * (2 * G) + (hd * G + g + 1))
                                nc.scalar.activation(wo_hi[:, g, :], wo_raw[:, g, :], ACT.Copy
                                                     ).then_inc(wo_hi_done, 1)
                        n = hd * NT + i
                        act.wait_ge(pv_done, it * BLOCKS + (block_index(hd, i, i) + 1 + PT))
                        act.wait_ge(y_done, it * UNITS + (n + 1))
                        nc.scalar.activation(o_hi[:, :], ps[:, O_BANK, :], ACT.Copy).then_inc(o_hi_done, 1)

            layer_norm(1, 2, 3, ln_f2)

            def hi_weights(n, m, par, width):
                act.wait_ge(wf_ready, n + 5)
                if n >= 4:
                    act.wait_ge(up_done, n // 2 * 2 - 2)
                nc.scalar.activation(gu_hi[:, par, m, :, 0:width],
                                     wf[:, m, 0:KT * width].rearrange("p (k n) -> p k n", k=KT), ACT.Copy
                                     ).then_inc(wf_hi, 1)

            def ffn_chunk(c, par, width, following):
                for half in range(2):
                    n = c * 2 + half
                    act.wait_ge(gate_done, n + 1)
                    if n >= 1:
                        act.wait_ge(silu_done, n)
                    nc.scalar.activation(sig[0:width, :], ps[0:width, 2 * (n % 4), :], ACT.Sigmoid
                                         ).then_inc(sig_done, 1)
                    if half == 0 and following:
                        for m in range(2):
                            hi_weights((c + 1) * 2 + m, m, 1 - par, following)
                    act.wait_ge(act_ready, n + 1)
                    nc.scalar.activation(t_hi[0:width, c, half * HALF:(half + 1) * HALF],
                                         act2[0:width, half, :], ACT.Copy).then_inc(act_hi, 1)

            for m in range(2):
                hi_weights(m, m, 0, P)
            for c in range(NC_FULL):
                ffn_chunk(c, c % 2, P, P if c + 1 < NC_FULL else C_LAST)
            ffn_chunk(NC_FULL, 0, C_LAST, 0)
            for c in range(NCH):
                n = P if c < NC_FULL else C_LAST
                act.wait_ge(wf_ready, 4 + 2 * NCH + c + 1)
                if c >= 2:
                    act.wait_ge(d_used, c - 1)
                nc.scalar.activation(d_hi[0:n, c % 2, :], wf[0:n, c % 2, :], ACT.Copy).then_inc(wf_hi, 1)
            for t in range(NT):
                act.wait_ge(y2_done, t + 1)
                if t >= 2:
                    act.wait_ge(fin_step, t - 1)
                nc.scalar.activation(o16[:, t % 2, :], ps[:, t, :], ACT.Copy).then_inc(o16_done, 1)

        @block.vector
        def _(dve):
            dve.sem_inc(wo_ready, 1)
            dve.sem_inc(proj_split, 1)
            dve.sem_inc(s_biased, 2)
            dve.sem_inc(pt_split, 2)
            dve.sem_inc(o_split, 1)
            dve.sem_inc(x_added, 1)
            dve.sem_inc(wf_ready, 4)
            dve.memset(eps_col[:, :], EPS).then_inc(silu_step, 1)

            dve.wait_ge(silu_exp, 1)
            dve.tensor_scalar(c_tmp[:, 1, :], c_tmp[:, 0, :], 1.0, None, ALU.add).then_inc(silu_step, 1)
            dve.wait_ge(silu_step, 2)
            dve.reciprocal(c_tmp[:, 2, :], c_tmp[:, 1, :]).then_inc(silu_step, 1)
            dve.wait_ge(silu_step, 3)
            dve.tensor_tensor(silu_c[:, :], c_col[:, :], c_tmp[:, 2, :], ALU.mult).then_inc(silu_step, 1)
            dve.wait_ge(silu_step, 4)
            dve.tensor_copy(silu_b[:, :, :], silu_c[:, :].unsqueeze(2).to_broadcast([P, KT, P])
                            ).then_inc(silu_ready, 1)

            def statistics(t):
                dve.bn_stats(stats[:, t, :], x[:, t, :]).then_inc(stat_step, 1)

            def aggregate(count):
                dve.wait_ge(stat_step, count)
                for t in range(NT):
                    dve.bn_aggr(moments[:, t, :], stats[:, t, :]).then_inc(stat_step, 1)
                dve.wait_ge(stat_step, count + NT)
                dve.sem_inc(var_ready, 1)

            def clamp(gate, size, value, count):
                dve.scalar_tensor_tensor(out=size, in0=value, scalar=-1.0, in1=value, op0=ALU.mult, op1=ALU.max
                                         ).then_inc(gate_step, 1)
                dve.wait_ge(gate_step, count + 1)
                dve.tensor_scalar(size, size, 0.25, None, ALU.max).then_inc(gate_step, 1)
                dve.tensor_scalar(value, value, 0.0, 2.0, ALU.is_ge, ALU.mult).then_inc(gate_step, 1)
                dve.wait_ge(gate_step, count + 3)
                dve.scalar_tensor_tensor(out=gate, in0=value, scalar=-1.0, in1=size, op0=ALU.add,
                                         op1=ALU.mult).then_inc(gate_step, 1)

            def normalise_rows(n, half, xn):
                for t in range(half * 4, half * 4 + 4):
                    if t >= 2:
                        dve.wait_ge(xn_moved, n * NT + t - 1)
                    dve.tensor_scalar(xn[:, t % 2, :], x[:, t, :], moments[:, t, 0:1], rstd[:, t:t + 1],
                                      ALU.subtract, ALU.mult).then_inc(xn_ready, 1)

            def split_rows(n, half, ln_f):
                tok = slice(half * HALF, (half + 1) * HALF)
                for f in range(KT):
                    k = half * KT + f
                    dve.wait_ge(ln_f_done, n * 2 * KT + k + 1)
                    dve.tensor_copy(h_hi[:, f, tok], ln_f[:, k % LNF, :]).then_inc(h_hi_done, 1)
                    if k % 2 == 0:
                        dve.wait_ge(h_hi_done, n * 2 * KT + k + 1)
                        dve.tensor_tensor(h_lo[:, f, tok], ln_f[:, k % LNF, :], r32(h_hi[:, f, tok]),
                                          ALU.subtract).then_inc(h_lo_dve, 1)

            def inverse_std(n, count):
                dve.wait_ge(std_ready, n + 1)
                dve.reciprocal(rstd[:, :], std[:, :]).then_inc(stat_step, 1)
                dve.wait_ge(stat_step, count)

            for t in range(NT):
                dve.wait_ge(x_in_sem[t], 16)
                statistics(t)
            aggregate(NT)
            inverse_std(0, 2 * NT + 1)
            normalise_rows(0, 0, xn)
            dve.wait_ge(mod_done, 1)
            dve.tensor_scalar(mod_cols[:, 0, :], ps[:, 4, 0:KT], 1.0, None, ALU.add).then_inc(gate_step, 1)
            dve.tensor_copy(mod_cols[:, 1, :], ps[:, 4, KT:2 * KT]).then_inc(gate_step, 1)
            dve.wait_ge(gate_step, 2)
            dve.sem_inc(cols_ready, 1)
            normalise_rows(0, 1, xn)
            split_rows(0, 0, ln_f)
            split_rows(0, 1, ln_f)
            dve.wait_ge(mod_done, 2)
            dve.tensor_copy(g_tmp[:, 0, :], ps[:, GATE_BANK, :]).then_inc(gate_row, 1)
            dve.wait_ge(gate_row, 1)
            clamp(gate_a[:, :], g_tmp[:, 1, :], g_tmp[:, 0, :], 2)
            dve.wait_ge(gate_step, 6)
            dve.sem_inc(gate_a_ready, 1)

            dve.wait_ge(consts_loaded, 48)
            with dve.Fori(0, PAIRS) as it:
                def project_lo(kind, hd, n, half):
                    G_i = group_index(kind, hd, n, half)
                    dve.wait_ge(proj_hi, it * NG + (G_i + 1))
                    bank = ps[:, G_i % 4 if G_i < len(HEAD_GROUPS) else M_BANK, :]
                    tok = slice(half * HALF, (half + 1) * HALF)
                    if kind == "q":
                        ins = dve.scalar_tensor_tensor(out=q_lo[:, n, tok], in0=bank,
                                                       scalar=consts[:, 0, hd, n:n + 1],
                                                       in1=r32(q_hi[:, n, tok]), op0=ALU.mult, op1=ALU.subtract)
                    elif kind == "k":
                        ins = dve.tensor_tensor(k_lo[:, tok], bank, r32(k_hi[:, tok]), ALU.subtract)
                    else:
                        ins = dve.tensor_tensor(v_lo[:, :, n, :],
                                                bank[:, 0:2 * D].rearrange("p (a d) -> p a d", a=2),
                                                r32(v_hi[:, :, n, :]), ALU.subtract)
                    ins.then_inc(proj_split, 1)

                def bias_and_minimum(hd, i, g, blocks_before):
                    n = (hd * NT + i) * G + g
                    dve.wait_ge(s_done, it * (UNITS * G) + (n + 1))
                    dve.wait_ge(t_done, it * BLOCKS + (blocks_before + 1))
                    alone(dve)
                    w = (i + 1) * P
                    bank = 2 * (g % 2)
                    dve.tensor_tensor_reduce(
                        out=probs[:, i % 2, g, 0:w],
                        in0=ps[:, bank:bank + 2, :].rearrange("p b n -> p (b n)")[:, 0:w],
                        in1=sdist[:, S - w:S], scale=1.0, scalar=3.0e38, op0=ALU.add, op1=ALU.min,
                        accum_out=low[:, i % 2, g:g + 1]).then_inc(s_biased, 1)
                    dve.wait_ge(s_biased, it * (UNITS * G) + (n + 3))
                    dve.tensor_tensor(shift[:, i % 2, g:g + 1], low[:, i % 2, g:g + 1],
                                      consts[:, 1, hd, g:g + 1], ALU.mult).then_inc(shift_ready, 1)

                def invert(hd, i, g):
                    dve.wait_ge(exp_done, it * (UNITS * G) + ((hd * NT + i) * G + g + 1))
                    dve.reciprocal(inv[:, i % 2, g:g + 1], rowsum[:, i % 2, g:g + 1]).then_inc(inv_ready, 1)

                def add_product(n):
                    i = n % NT
                    if n > NT:
                        dve.wait_ge(x_added, it * UNITS + (n + 1))
                        statistics(i - 1)
                    dve.wait_ge(y_done, it * UNITS + (n + 2))
                    dve.tensor_tensor(x[:, i, :], ps[:, M_BANK, :], x[:, i, :], ALU.add).then_inc(x_added, 1)

                dve.tensor_copy(consts[:, :, :, :], table[:, bass.ds(it, 1), :, :, :].rearrange(
                    "p a c h g -> p (a c) h g")).then_inc(head_consts, 1)
                dve.wait_ge(head_consts, it + 1)
                for grp in HEAD_GROUPS:
                    project_lo(*grp)
                for g in range(G):
                    bias_and_minimum(A, 0, g, 0)
                for g in range(G):
                    invert(A, 0, g)
                for hd in range(2):
                    for i in range(NT):
                        nxt = next_unit(hd, i)
                        waiting, exps = [], []
                        for s in slots(i):
                            if s <= i:
                                b = block_index(hd, i, s)
                                dve.wait_ge(pt_hi_done, it * BLOCKS + (b + 1))
                                dve.tensor_tensor(pt_lo[:, b % PT, :], ps[:, T_BANK + b % 2, :],
                                                  r32(pt_hi[:, b % PT, :]), ALU.subtract).then_inc(pt_split, 1)
                            for slot, grp, _u in FILL.get((hd, i), []):
                                if slot == s:
                                    project_lo(*grp)
                            if nxt:
                                fresh = [g for g in range(G) if score_slots(hd, i)[g] == s]
                                for g in fresh:
                                    bias_and_minimum(*nxt, g, block_index(hd, i, 0))
                                for g in waiting:
                                    invert(*nxt, g)
                                waiting = fresh
                            if s == wo_slot(hd, i) and i > 0:
                                add_product(hd * NT + i - 1)
                            elif s == wo_slot(hd, i) and hd == B:
                                add_product(NT - 1)
                        for g in waiting:
                            invert(*nxt, g)
                        if i == 0:
                            for g in range(G):
                                dve.wait_ge(wo_hi_done, it * (2 * G) + (hd * G + g + 1))
                                ins = dve.tensor_tensor(wo_lo[:, g, :], wo_raw[:, g, :], r32(wo_hi[:, g, :]),
                                                        ALU.subtract)
                                ins.then_inc(wo_ready, 1)
                        n = hd * NT + i
                        dve.wait_ge(o_hi_done, it * UNITS + (n + 1))
                        dve.tensor_tensor(o_lo[:, :], ps[:, O_BANK, :], r32(o_hi[:, :]), ALU.subtract
                                          ).then_inc(o_split, 1)
                add_product(UNITS - 1)

            dve.wait_ge(x_added, PAIRS * UNITS + 1)
            statistics(NT - 1)
            total = 2 * NT + 1 + PAIRS * (NT - 1) + 1
            aggregate(total)
            inverse_std(1, total + NT + 1)
            dve.tensor_copy(silu_b2[:, :, :], silu_c[:, :].unsqueeze(2).to_broadcast([P, KT, P])
                            ).then_inc(silu_ready, 1)
            normalise_rows(1, 0, xn2)
            dve.wait_ge(mod_done, 3)
            dve.tensor_scalar(mod_cols[:, 2, :], ps[:, T_BANK, 0:KT], 1.0, None, ALU.add).then_inc(gate_step, 1)
            dve.tensor_copy(mod_cols[:, 3, :], ps[:, T_BANK, KT:2 * KT]).then_inc(gate_step, 1)
            dve.wait_ge(gate_step, 8)
            dve.sem_inc(cols_ready, 1)
            dve.wait_ge(mod_done, 4)
            dve.tensor_copy(gate_b[:, :], ps[:, T_BANK + 1, :]).then_inc(gate_row, 1)
            normalise_rows(1, 1, xn2)
            split_rows(1, 0, ln_f2)

            dve.wait_ge(shifts_loaded, 16)

            def dequantise(n, q, z, s, w, groups, rows, loaded, count, buffer_free):
                width = q.shape[-1]
                k = n_dq[0]
                n_dq[0] += 1
                dve.wait_ge(loaded, count)
                size = groups * width
                nv = nib[0:rows, 0:size].rearrange("p (k n) -> p k n", k=groups)
                zv = znib[0:rows, 0, 0:size]
                zm = znib[0:rows, 1, 0:size]
                dve.wait_ge(wf_ready, 4 + k)
                if buffer_free:
                    buffer_free()
                dve.tensor_scalar(nv, q, shifts[0:rows, 0:1], 15, ALU.logical_shift_right, ALU.bitwise_and
                                  ).then_inc(dq_step, 1)
                z4d = z.unsqueeze(3).to_broadcast([rows, groups, width // PACK, PACK])
                sh = shifts[0:rows, 1:1 + PACK].unsqueeze(1).unsqueeze(1).to_broadcast(
                    [rows, groups, width // PACK, PACK])
                dve.tensor_tensor(zv.rearrange("p (k a b) -> p k a b", k=groups, b=PACK), z4d, sh,
                                  ALU.logical_shift_right).then_inc(dq_step, 1)
                dve.wait_ge(dq_step, 4 * k + 2)
                dve.tensor_scalar(zm, zv, 15, None, ALU.bitwise_and).then_inc(dq_step, 1)
                dve.wait_ge(dq_step, 4 * k + 3)
                dve.tensor_tensor(dif[0:rows, 0:size], nib[0:rows, 0:size], zm, ALU.subtract).then_inc(dq_step, 1)
                dve.wait_ge(dq_step, 4 * k + 4)
                dve.scalar_tensor_tensor(out=w[0:rows, 0:size].rearrange("p (k n) -> p k n", k=groups),
                                         in0=dif[0:rows, 0:size].rearrange("p (k n) -> p k n", k=groups),
                                         scalar=-1.0, in1=s, op0=ALU.add, op1=ALU.mult).then_inc(wf_ready, 1)

            n_dq = [0]

            def dequantise_gu(c, par, width):
                for m in range(2):
                    n = 2 * c + m
                    dequantise(n, q4[:, par, m, :, 0:width], z4[:, par, m, :, 0:width // PACK],
                               s4[:, par, m, :, 0:width], wf[:, m, :], KT, P, gu_loaded[par],
                               (c // 2 + 1) * 16 * 2 * (KT + 2),
                               (lambda: dve.wait_ge(wf_split, n - 1)) if n >= 2 else None)

            def ffn_chunk(c, par, width, following):
                for half in range(2):
                    n = c * 2 + half
                    dve.wait_ge(sig_done, n + 1)
                    if n >= 1:
                        dve.wait_ge(act_ready, n)
                    dve.tensor_tensor(act1[0:width, :], ps[0:width, 2 * (n % 4), :], sig[0:width, :], ALU.mult
                                      ).then_inc(silu_done, 1)
                    dve.wait_ge(silu_done, n + 1)
                    dve.wait_ge(up_done, n + 1)
                    if n >= 2:
                        dve.wait_ge(act_split, n - 1)
                    dve.tensor_tensor(act2[0:width, half, :], ps[0:width, 2 * (n % 4) + 1, :],
                                      act1[0:width, :], ALU.mult).then_inc(act_ready, 1)

            dequantise_gu(0, 0, P)
            split_rows(1, 1, ln_f2)
            for c in range(NCH):
                width = P if c < NC_FULL else C_LAST
                if c + 1 < NCH:
                    dequantise_gu(c + 1, (c + 1) % 2, P if c + 1 < NC_FULL else C_LAST)
                ffn_chunk(c, c % 2, width, 0)
            for c in range(NCH):
                n = P if c < NC_FULL else C_LAST
                def free(c=c):
                    dve.wait_ge(wf_split, 2 * NCH + c - 1)
                dequantise(2 * NCH + c, qd[0:n, c % 2, :].unsqueeze(1), zd[0:n, c % 2, :].unsqueeze(1),
                           sd[0:n, c % 2, :].unsqueeze(1), wf[:, c % 2, :], 1, n, d_loaded[c % 2],
                           (c // 2 + 1) * 48, free)
            clamp(gate_b[:, :], gate_size[:, :], gate_b[:, :], 8)
            dve.wait_ge(gate_step, 12)
            for t in range(NT):
                dve.wait_ge(o16_done, t + 1)
                if t >= 2:
                    dve.wait_ge(out_stored[t % 2], 16 * (t // 2))
                dve.tensor_tensor(fin[:, t % 2, :], o16[:, t % 2, :], gate_b[:, :], ALU.mult).then_inc(fin_step, 1)
                dve.wait_ge(fin_step, t + 1)
                dve.tensor_tensor(fin[:, t % 2, :], fin[:, t % 2, :], x[:, t, :], ALU.add).then_inc(fin_ready, 1)

        @block.tensor
        def _(pe):
            pe.sem_inc(proj_done, 1)
            pe.sem_inc(t_done, 1)
            pe.sem_inc(pv_done, PT)
            pe.sem_inc(y_done, 1)

            def products(out_ap, terms, done=None):
                for n, (l_hi, l_lo, r_hi, r_lo) in enumerate(terms):
                    pe.matmul(out_ap, l_hi, r_hi, start=(n == 0), stop=False)
                    pe.matmul(out_ap, l_hi, r_lo, start=False, stop=False)
                    ins = pe.matmul(out_ap, l_lo, r_hi, start=False, stop=(n == len(terms) - 1))
                return ins

            def modulation_columns(w, which, bank):
                for j, m in enumerate(which):
                    pe.wait_ge(mod_loaded[m], 16)
                    for f in range(KT):
                        for k in range(KT):
                            ins = pe.matmul(ps[:, bank, j * KT + f:j * KT + f + 1], w[:, j, k, f * P:(f + 1) * P],
                                            silu_c[:, k:k + 1], start=(k == 0), stop=(k == KT - 1))
                ins.then_inc(mod_done, 1)

            def modulation_rows(w, m, bank, silu_b):
                pe.wait_ge(mod_loaded[m], 16)
                for k in range(KT):
                    ins = pe.matmul(ps[:, bank, :], silu_b[:, k, :], w[:, 2, k, :],
                                    start=(k == 0), stop=(k == KT - 1))
                ins.then_inc(mod_done, 1)

            def transpose_rows(n, half, xn):
                for t in range(half * 4, half * 4 + 4):
                    pe.wait_ge(xn_ready, n * NT + t + 1)
                    for f in range(KT):
                        c = (t % 4) * P
                        ins = pe.transpose(ps[:, LN_BANK(half, f), c:c + P], xn[:, t % 2, f * P:(f + 1) * P],
                                           ident[:, :])
                    ins.then_inc(xn_moved, 1)

            def wait_h(n, half):
                for k in (half * KT + KT - 2, half * KT + KT - 1):
                    pe.wait_ge(*h_lo_done(n, k))

            pe.wait_ge(silu_ready, 1)
            modulation_columns(wmod, (1, 0), 4)
            pe.wait_ge(consts_loaded, 48)
            transpose_rows(0, 0, xn)
            pe.wait_ge(cols_ready, 1)
            transpose_rows(0, 1, xn)
            wait_h(0, 0)
            modulation_rows(wmod, 2, GATE_BANK, silu_b)
            wait_h(0, 1)
            pe.wait_ge(gate_row, 1)

            with pe.Fori(0, PAIRS) as it:
                def project(kind, hd, n, half, use):
                    G_i = group_index(kind, hd, n, half)
                    in_head = G_i < len(HEAD_GROUPS)
                    if in_head and G_i < 4:
                        pe.wait_ge(s_biased, it * (UNITS * G) + (1 + G_i // 2))
                    elif in_head:
                        pe.wait_ge(proj_split, it * NG + (G_i - 4 + 2))
                    else:
                        pe.wait_ge(proj_split, it * NG + (G_i + 1))
                    bank = ps[:, G_i % 4 if in_head else M_BANK, :]
                    tok = slice(half * HALF, (half + 1) * HALF)
                    slot = use % RING
                    if kind == "v":
                        pe.wait_ge(w_ready, it * NU + (use + 2 + RING))
                        tt = slice(n * P, (n + 1) * P)
                        ins = products(bank[:, 0:2 * D],
                                       [(h_hi[:, k, tt], h_lo[:, k, tt], w_hi[:, slot:slot + 2, k, :],
                                         w_lo[:, slot:slot + 2, k, :]) for k in range(KT)])
                    else:
                        pe.wait_ge(w_ready, it * NU + (use + 1 + RING))
                        ins = products(bank, [(w_hi[:, slot, k, :], w_lo[:, slot, k, :], h_hi[:, k, tok],
                                               h_lo[:, k, tok]) for k in range(KT)])
                    ins.then_inc(proj_done, 1)

                def score(hd, i, g):
                    n = (hd * NT + i) * G + g
                    half = i // 4
                    need = max(group_index("q", hd, g, half), group_index("k", hd, 0, 1))
                    if n == 0 or n == 1:
                        need = len(HEAD_GROUPS) - 1
                    pe.wait_ge(proj_split, it * NG + (need + 2))
                    pe.wait_ge(s_biased, it * (UNITS * G) + (n + 1))
                    lo = slice(i * P, (i + 1) * P)
                    for b, width in enumerate(score_banks(i)):
                        keys = slice(b * 512, b * 512 + width)
                        ins = products(ps[:, 2 * (g % 2) + b, 0:width],
                                       [(q_hi[:, g, lo], q_lo[:, g, lo], k_hi[:, keys], k_lo[:, keys])])
                    ins.then_inc(s_done, 1)

                def transpose_block(hd, i, s):
                    b = block_index(hd, i, s)
                    pe.wait_ge(pt_split, it * BLOCKS + (b + 1))
                    for g in range(G):
                        if s == 0:
                            pe.wait_ge(normed, it * (UNITS * G) + ((hd * NT + i) * G + g + 1))
                        ins = pe.transpose(ps[:, T_BANK + b % 2, g * P:(g + 1) * P],
                                           probs[:, i % 2, g, s * P:(s + 1) * P], ident[:, :])
                    ins.then_inc(t_done, 1)

                def attend(hd, i, s):
                    b = block_index(hd, i, s)
                    pe.wait_ge(pt_split, it * BLOCKS + (b + 3))
                    if s == 0:
                        pe.wait_ge(o_split, it * UNITS + (hd * NT + i + 1))
                    o, v1, v2 = ps[:, O_BANK, :], v_hi[:, hd, s, :], v_lo[:, hd, s, :]
                    p1, p2 = pt_hi[:, b % PT, :], pt_lo[:, b % PT, :]
                    pe.matmul(o, v1, p1, start=(s == 0), stop=False)
                    pe.matmul(o, v1, p2, start=False, stop=False)
                    ins = pe.matmul(o, v2, p1, start=False, stop=(s == i))
                    ins.then_inc(pv_done, 1)
                    return ins

                def output_product(n, groups_before):
                    pe.wait_ge(o_split, it * UNITS + (n + 2))
                    pe.wait_ge(wo_ready, it * (2 * G) + ((n // NT + 1) * G + 1))
                    pe.wait_ge(x_added, it * UNITS + (n + 1))
                    pe.wait_ge(proj_split, it * NG + (groups_before + 1))
                    cols = [slice(g * P, (g + 1) * P) for g in range(G)]
                    products(ps[:, M_BANK, :], [(o_hi[:, cols[g]], o_lo[:, cols[g]], wo_hi[:, g, :], wo_lo[:, g, :])
                                                for g in range(G)]).then_inc(y_done, 1)

                done = 0
                u_of = [0, 0] + [1] * NT + [3, 4, 5, 6]
                for j, grp in enumerate(HEAD_GROUPS):
                    project(*grp, u_of[j])
                    done += 1
                for g in range(G):
                    score(A, 0, g)
                for hd in range(2):
                    for i in range(NT):
                        n = hd * NT + i
                        nxt = next_unit(hd, i)
                        for s in slots(i):
                            if s <= i:
                                transpose_block(hd, i, s)
                            for slot, grp, use in FILL.get((hd, i), []):
                                if slot == s:
                                    pe.wait_ge(x_added, it * UNITS + max(n, 1))
                                    project(*grp, use)
                                    done += 1
                            if nxt:
                                for g in range(G):
                                    if score_slots(hd, i)[g] == s:
                                        score(*nxt, g)
                            if s == wo_slot(hd, i) and n > 0:
                                output_product(n - 1, done)
                            if s >= LAG:
                                attend(hd, i, s - LAG)
                output_product(UNITS - 1, done)

            pe.wait_ge(pt_split, PAIRS * BLOCKS + 2)
            modulation_columns(wmod2, (4, 3), T_BANK)
            transpose_rows(1, 0, xn2)
            pe.wait_ge(silu_ready, 2)
            modulation_rows(wmod2, 5, T_BANK + 1, silu_b2)
            pe.wait_ge(cols_ready, 2)
            pe.wait_ge(gate_row, 2)
            transpose_rows(1, 1, xn2)

            for c in range(NCH):
                width, par = (P if c < NC_FULL else C_LAST), c % 2
                pe.wait_ge(wf_split, 2 * c + 2)
                for half in range(2):
                    n = 2 * c + half
                    tok = slice(half * HALF, (half + 1) * HALF)
                    if c == 0:
                        wait_h(1, half)
                    if n >= 4:
                        pe.wait_ge(act_ready, n - 3)
                    for m, done in ((0, gate_done), (1, up_done)):
                        products(ps[0:width, 2 * (n % 4) + m, :],
                                 [(gu_hi[:, par, m, k, 0:width], gu_lo[:, par, m, k, 0:width],
                                   h_hi[:, k, tok], h_lo[:, k, tok]) for k in range(KT)]).then_inc(done, 1)
            pe.wait_ge(act_ready, 2 * NCH)
            pe.wait_ge(act_split, 2 * NCH)
            for c in range(NCH):
                rows, par = (P if c < NC_FULL else C_LAST), c % 2
                pe.wait_ge(wf_split, 2 * NCH + c + 1)
                for t in range(NT):
                    tok = slice(t * P, (t + 1) * P)
                    l1, l2, r1, r2 = t_hi[0:rows, c, tok], t_lo[0:rows, c, tok], d_hi[0:rows, par, :], d_lo[0:rows, par, :]
                    pe.matmul(ps[:, t, :], l1, r1, start=(c == 0), stop=False)
                    pe.matmul(ps[:, t, :], l1, r2, start=False, stop=False)
                    ins = pe.matmul(ps[:, t, :], l2, r1, start=False, stop=(c == NCH - 1))
                    if c == NCH - 1:
                        ins.then_inc(y2_done, 1)
                if c < NCH - 1:
                    ins.then_inc(d_used, 1)


def kernel(**inputs):
    import numpy as _np
    import concourse.bacc as _bacc
    from concourse import mybir as _mybir
    from concourse.bass_utils import run_bass_kernel_spmd as _run

    nc = _bacc.Bacc("TRN2", target_bir_lowering=False, num_devices=1)
    arrays = {}

    def dram(name, a):
        a = _np.ascontiguousarray(a)
        arrays[name] = a
        return nc.dram_tensor(name, a.shape, _mybir.dt.from_np(a.dtype), kind="ExternalInput").ap()

    p = _np.arange(P)[:, None]
    rel = p + (S - P) - _np.arange(S)[None, :]
    sqrt_dist = _np.where(rel >= 0, _np.sqrt(_np.maximum(rel, 0).astype(_np.float32)),
                          _np.float32(MASKED)).astype(_np.float32)
    slope_base = 2.0 ** (-8.0 / NH)
    slopes = (slope_base ** _np.arange(1, NH + 1, dtype=_np.float32)).astype(_np.float32)
    per_head = slopes.reshape(PAIRS, 1, 2, G)
    table = _np.concatenate([-_np.float32(D ** -0.5) / per_head, per_head, -per_head], axis=1)
    table = _np.broadcast_to(table[None], (P,) + table.shape).astype(_np.float32)
    shifts = _np.concatenate([_np.broadcast_to(4 * (p % PACK), (P, 1)),
                              _np.broadcast_to(4 * _np.arange(PACK), (P, PACK))], axis=1).astype(_np.int32)

    args = [
        dram("x_dram", inputs["L0_attn_hidden_states"][0]),
        dram("w_qkv_dram", inputs["L0_attn_w_qkv"]),
        dram("w_o_dram", inputs["L0_attn_w_o"]),
        [dram(f"{m}_q_dram", inputs[f"L0_ffn_{m}_qweight"]) for m in ("gate", "up", "down")],
        [dram(f"{m}_s_dram", inputs[f"L0_ffn_{m}_scales"]) for m in ("gate", "up", "down")],
        [dram(f"{m}_z_dram", inputs[f"L0_ffn_{m}_zeros"]) for m in ("gate", "up", "down")],
        dram("c_dram", _np.asarray(inputs["L0_c"]).reshape(KT, P).T),
        dram("w_mod_dram", inputs["L0_wmod"]),
        dram("sqrt_dist_dram", sqrt_dist),
        dram("head_table_dram", table),
        dram("ident_dram", _np.eye(P, dtype=_np.float32)),
        dram("shifts_dram", shifts),
        nc.dram_tensor("out_dram", (S, H), F32, kind="ExternalOutput").ap(),
    ]
    build(nc, *args)
    r = _run(nc, [arrays], core_ids=[0])
    return r.results[0]["out_dram"].reshape(1, S, H)
```

```python
import numpy as np
import concourse.bass as bass
from concourse import mybir

F32 = mybir.dt.float32
F32R = mybir.dt.float32r
F16 = mybir.dt.float16
I32 = mybir.dt.int32
ALU = mybir.AluOpType
ACT = mybir.ActivationFunctionType

P = 128
S = 1024
H = 512
NH, NKV, D = 32, 8, 128
G = NH // NKV
NT = S // P
KT = H // P
HALF = 512
INTER = 1376
PACK = 8
NC_FULL, C_LAST = INTER // P, INTER % P
NCH = NC_FULL + 1
FFN_PAIRS = NC_FULL // 2 - 1
ROWS = P // PACK
MASKED = 1.0e30
EPS = 1e-5

PAIRS = NKV // 2
UNITS = 2 * NT
BLOCKS = NT * (NT + 1)

A, B = 0, 1
GATE_BANK = 0
GATE_B_BANK = 3
WARM_UP = 10
MOD_BANK = 6
T_BANK, O_BANK, M_BANK = 4, 6, 7
USES = ([("q", A, g) for g in range(G - 1)] + [("k", A, 0), ("v", A, 0), ("v", B, 0), ("q", A, G - 1)]
        + [("q", A, g) for g in range(G)] + [("q", B, g) for g in range(G)] + [("k", B, 0)]
        + [("q", B, g) for g in range(G)])
NU = len(USES)
RING = 4
LAG = 2
NORM_PARTS = [[slice(0, 4), slice(4, 8)], [slice(0, 8)]]
FINB = 4
XNB = 4
LNF = 4
PT = 3
USE_QA1, USE_QB0, USE_KB, USE_QB1 = 7, 11, 15, 16
HEAD_GROUPS = ([("q", A, g, 0) for g in range(G - 1)]
               + [("k", A, 0, 0), ("v", A, 0, 0), ("v", A, 1, 0), ("q", A, G - 1, 0), ("v", A, 2, 0), ("v", A, 3, 0),
                  ("k", A, 0, 1)] + [("v", A, t, 0) for t in range(4, NT)])
HEAD_USES = [USES.index((kind, A, 0 if kind == "v" else n)) for kind, _hd, n, _half in HEAD_GROUPS]
HEAD_BANKS = (4, 5, 6)
SCORES_AFTER = [5, 7, 8, 9]
FIRST_SLOT = 2
KB_SLOTS = (3, 5)
FILL = {}
for _i in range(G):
    FILL[(A, _i)] = [(FIRST_SLOT if _i == 0 else 0, ("q", A, _i, 1), USE_QA1 + _i)]
    FILL[(A, G + _i)] = [(0, ("q", B, _i, 0), USE_QB0 + _i)]
    FILL[(B, _i)] = [(FIRST_SLOT if _i == 0 else 0, ("q", B, _i, 1), USE_QB1 + _i)]
FILL[(A, NT - 1)] += [(KB_SLOTS[0], ("k", B, 0, 0), USE_KB), (KB_SLOTS[1], ("k", B, 0, 1), USE_KB)]
WO_AFTER = {6: [0], 8: [1], 9: [2], 10: [3]}
WO_SLOTS = {(B, 0, 1): [0, 1], (B, 1, 0): [2, 3]}
GROUPS = HEAD_GROUPS + [f[1] for hd in range(2) for i in range(NT) for f in FILL.get((hd, i), [])]
NG = len(GROUPS)


LAST_GROUP = []
for _u, (_k, _hd, _g) in enumerate(USES):
    _of = [n for n, (k, hd, m, half) in enumerate(GROUPS)
           if k == _k and (k == "v" or hd == _hd) and (k != "q" or m == _g)]
    if _k == "q":
        _of = [_of[0 if _u < USE_QA1 or _u in range(USE_QB0, USE_KB) else 1]]
    LAST_GROUP.append(max(_of))


def group_index(kind, hd, n, half):
    return GROUPS.index((kind, hd, n, half))


def block_index(hd, i, s):
    return hd * (BLOCKS // 2) + i * (i + 1) // 2 + s


def score_slots(hd, i):
    if hd == A and i == NT - 1:
        return [5, 6, 7, 7]
    return {0: [0, 0, 1, 1], 1: [0, 0, 1, 2], 4: [0, 1, 3, 4], 5: [0, 1, 3, 4], 6: [0, 2, 3, 5]}.get(i, [0, 1, 2, 3])


def wo_slot(hd, i):
    return i + 1 if i > 0 else 0


def slots(i):
    return range(i + 1 + LAG)


def uses_of(unit):
    return sorted({f[2] for f in FILL.get(unit, [])}) if unit else []


def next_unit(hd, i):
    if i + 1 < NT:
        return hd, i + 1
    return (B, 0) if hd == A else None


def group_bank(n):
    return HEAD_BANKS[n % len(HEAD_BANKS)] if n < len(HEAD_GROUPS) else M_BANK


def product_bank(n):
    return M_BANK if n < UNITS - 1 else 0


def score_width(i):
    return (i + 1) * P if i < 4 else (i + 1) * P // 2


def build(nc, x_in, w_qkv, w_o, qw, sc, zr, c_in, w_mod, sqrt_dist, head_table, ident_in, shift_in, out):
    at = [((nc.sbuf_base if not callable(nc.sbuf_base) else nc.sbuf_base()) + 63) // 64 * 64]

    def place(name, shape, dtype, offset=None):
        size = int(np.prod(shape[1:])) * mybir.dt.size(dtype)
        where = at[0] if offset is None else offset
        if offset is None:
            at[0] += (size + 31) // 32 * 32
        return nc.alloc_sbuf_tensor_at(name, shape, dtype, offset=where)

    x = place("x", [P, NT, H], F32)
    h_hi = place("h_hi", [P, KT, S], F32R)
    h_lo = place("h_lo", [P, KT, S], F32R)
    ident = place("ident", [P, P], F32)
    mod_cols = place("mod_cols", [P, 4, KT], F32)
    stats = place("stats", [P, NT, 6], F32)
    moments = place("moments", [P, NT, 2], F32)
    std = place("std", [P, NT], F32)
    rstd = place("rstd", [P, NT], F32)
    eps_col = place("eps_col", [P, 1], F32)
    silu_c = place("silu_c", [P, KT], F32)
    base = at[0]

    q_hi = place("q_hi", [P, G, S], F32R)
    q_lo = place("q_lo", [P, G, S], F32R)
    k_hi = place("k_hi", [P, S], F32R)
    k_lo = place("k_lo", [P, S], F32R)
    v_hi = place("v_hi", [P, 2, NT, D], F32R)
    v_lo = place("v_lo", [P, 2, NT, D], F32R)
    probs_at = at[0]
    probs = place("probs", [P, 2, G, S], F32)
    pt_hi = place("pt_hi", [P, PT, G * P], F32R)
    pt_lo = place("pt_lo", [P, PT, G * P], F32R)
    o_hi = place("o_hi", [P, G * P], F32R)
    o_lo = place("o_lo", [P, G * P], F32R)
    assert (NT - 2) % 2 == 0
    last_o_hi = place("last_o_hi", [P, G * P], F32R, probs_at)
    last_o_lo = place("last_o_lo", [P, G * P], F32R, probs_at + G * P * 4)
    ring_at = at[0]
    w_raw = place("w_raw", [P, RING, KT, P], F32)
    w_hi = place("w_hi", [P, RING, KT, P], F32R)
    w_lo = place("w_lo", [P, RING, KT, P], F32R)
    wo_raw_at = at[0]
    wo_raw = place("wo_raw", [P, G, H], F32)
    wo_hi = place("wo_hi", [P, G, H], F32R)
    wo_lo = place("wo_lo", [P, G, H], F32R)
    sdist = place("sdist", [P, S], F32)
    gate_a = place("gate_a", [P, H], F32)
    table = place("table", [P, PAIRS, 3, 2, G], F32)
    consts = place("consts", [P, 3, 2, G], F32)
    low = place("low", [P, 2, G], F32)
    shift = place("shift", [P, 2, G], F32)
    rowsum = place("rowsum", [P, 2, G], F32)
    inv = place("inv", [P, 2, G], F32)
    assert at[0] <= (nc.sbuf_usable_end() if callable(nc.sbuf_usable_end) else nc.sbuf_usable_end), at[0]

    at[0] = base
    wmod = place("wmod", [P, 3, KT, H], F32)
    xn = place("xn", [P, XNB, H], F32)
    ln_f = place("ln_f", [P, LNF, HALF], F32)
    c_col = place("c_col", [P, KT], F32)
    c_tmp = place("c_tmp", [P, 3, KT], F32)
    silu_b = place("silu_b", [P, KT, P], F32)
    g_tmp = place("g_tmp", [P, 2, H], F32)
    mod_rows = place("mod_rows", [1, 2, H], F32)

    at[0] = base
    wmod2 = place("wmod2", [P, 3, KT, H], F32, base)
    silu_b2 = place("silu_b2", [P, KT, P], F32, base + 3 * KT * H * 4)
    mod_rows2 = place("mod_rows2", [1, 2, H], F32, base + 3 * KT * H * 4 + KT * P * 4)
    t_hi = place("t_hi", [P, NCH, S], F32R)
    t_lo = place("t_lo", [P, NCH, S], F32R)
    ln_f2_at = at[0] - LNF * HALF * 4
    ln_f2 = place("ln_f2", [P, LNF, HALF], F32, ln_f2_at)
    xn2 = place("xn2", [P, XNB, H], F32, ln_f2_at - XNB * H * 4)
    gu_at = at[0]
    gu_hi = place("gu_hi", [P, 2, 2, KT, P], F32R)
    gu_lo = place("gu_lo", [P, 2, 2, KT, P], F32R)
    assert at[0] <= ring_at
    at[0] = ring_at
    s4 = place("s4", [P, 2, 2, KT, P], F16)
    z4 = place("z4", [P, 2, 2, KT, P // PACK], I32)
    nib = place("nib", [P, KT * P], I32)
    znib = place("znib", [P, 2, KT * P], I32)
    dif = place("dif", [P, KT * P], F32)
    wf = place("wf", [P, 2, KT * P], F32)
    shifts = place("shifts", [P, 1 + PACK], I32)
    sig = place("sig", [P, HALF], F32)
    act1 = place("act1", [P, HALF], F32)
    o16 = place("o16", [P, 2, H], F16)
    assert at[0] <= wo_raw_at
    at[0] = wo_raw_at
    q4 = place("q4", [P, 2, 2, KT, P], I32)
    act2 = place("act2", [P, 2, HALF], F32)
    qd = place("qd", [P, 2, H], I32)
    sd = place("sd", [P, 2, H], F16)
    zd = place("zd", [P, 2, H // PACK], I32)
    d_hi = place("d_hi", [P, 2, H], F32R)
    d_lo = place("d_lo", [P, 2, H], F32R)
    gate_b = place("gate_b", [P, H], F32)
    gate_size = place("gate_size", [P, H], F32)
    fin = place("fin", [P, FINB, H], F32, gu_at)
    last_d_hi = place("last_d_hi", [P, H], F32R, gu_at + FINB * H * 4)
    last_d_lo = place("last_d_lo", [P, H], F32R, gu_at + (FINB + 1) * H * 4)
    assert at[0] <= (nc.sbuf_usable_end() if callable(nc.sbuf_usable_end) else nc.sbuf_usable_end), at[0]

    ps = nc.alloc_psum_tensor("ps", [P, 8, 512], F32)

    def r32(ap):
        return ap.bitcast(F32)

    sem = lambda name: nc.alloc_semaphore(name)
    waits_passed = sem("waits_passed")
    x_in_sem = [sem(f"x_loaded{t}") for t in range(NT)]
    c_loaded = sem("c_loaded")
    consts_loaded = sem("consts_loaded")
    mod_loaded = [sem(f"mod_loaded{m}") for m in range(6)]
    silu_step = sem("silu_step")
    silu_exp = sem("silu_exp")
    silu_ready = sem("silu_ready")
    mod_row_done = sem("mod_row_done")
    mod_row_moved = sem("mod_row_moved")
    mod_done = sem("mod_done")
    ident_loaded = sem("ident_loaded")
    cols_ready = sem("cols_ready")
    gate_a_ready = sem("gate_a_ready")
    gate_row = sem("gate_row")
    gate_step = sem("gate_step")
    stat_step = sem("stat_step")
    var_ready = sem("var_ready")
    std_ready = sem("std_ready")
    xn_ready = sem("xn_ready")
    xn_moved = sem("xn_moved")
    ln_f_done = sem("ln_f_done")
    h_hi_done = sem("h_hi_done")
    h_lo_dve = sem("h_lo_dve")
    h_lo_pool = sem("h_lo_pool")
    w_loaded = [sem(f"w_loaded{i}") for i in range(RING)]
    w_hi_done = sem("w_hi_done")
    w_ready = sem("w_ready")
    wo_loaded = sem("wo_loaded")
    wo_scaled = sem("wo_scaled")
    wo_hi_done = sem("wo_hi_done")
    wo_ready = sem("wo_ready")
    head_consts = sem("head_consts")
    proj_done = sem("proj_done")
    proj_hi = sem("proj_hi")
    proj_split = sem("proj_split")
    s_done = sem("s_done")
    s_biased = sem("s_biased")
    shift_ready = sem("shift_ready")
    exp_done = sem("exp_done")
    inv_ready = sem("inv_ready")
    normed = sem("normed")
    t_done = sem("t_done")
    pt_hi_done = sem("pt_hi_done")
    pt_split = sem("pt_split")
    pv_done = sem("pv_done")
    o_hi_done = sem("o_hi_done")
    o_split = sem("o_split")
    y_done = sem("y_done")
    x_added = sem("x_added")
    shifts_loaded = sem("shifts_loaded")
    gu_loaded = [sem(f"gu_loaded{i}") for i in range(2)]
    dq_step = sem("dq_step")
    wf_ready = sem("wf_ready")
    wf_hi = sem("wf_hi")
    wf_split = sem("wf_split")
    gate_done = sem("gate_done")
    up_done = sem("up_done")
    sig_done = sem("sig_done")
    silu_done = sem("silu_done")
    act_ready = sem("act_ready")
    act_hi = sem("act_hi")
    act_split = sem("act_split")
    d_loaded = [sem(f"d_loaded{i}") for i in range(2)]
    d_used = sem("d_used")
    y2_done = sem("y2_done")
    o16_done = sem("o16_done")
    fin_step = sem("fin_step")
    fin_ready = sem("fin_ready")
    out_stored = [sem(f"out_stored{i}") for i in range(FINB)]

    def alone(eng):
        eng.sem_inc(waits_passed, 1)

    def o_parts(n):
        return (o_hi, o_lo) if n < UNITS - 1 else (last_o_hi, last_o_lo)

    def d_parts(c):
        return (d_hi[:, c % 2, :], d_lo[:, c % 2, :]) if c < NCH - 1 else (last_d_hi, last_d_lo)

    W3 = w_qkv.rearrange("(k p) n -> p k n", p=P)

    def use_columns(u, it):
        kind, hd, g = USES[u]
        if kind == "q":
            return it * (2 * G * D) + (hd * G + g) * D
        return it * (2 * D) + (NH * D + (NKV * D if kind == "v" else 0) + hd * D)

    def h_lo_done(n, k):
        if n == 0:
            return h_lo_dve, k + 1
        return (h_lo_pool, k // 2 + 1) if k % 2 else (h_lo_dve, 2 * KT + k // 2 + 1)

    LN_BANK = lambda half, f: half * KT + f

    block = nc.Block()
    with block:

        @block.sync
        def _(sp):
            for t in range(NT):
                if t == NT // 2:
                    sp.wait_ge(mod_loaded[1], 16)
                sp.dma_start(x[:, t, :], x_in[t * P:(t + 1) * P, :]).then_inc(x_in_sem[t], 16)
            wm = w_mod.rearrange("(k p) (m n) -> p m k n", p=P, m=6)
            with sp.Fori(0, PAIRS) as it:
                def load_wo(hd):
                    sp.wait_ge(wo_ready, (it * 2 + hd) * G + 1)
                    alone(sp)
                    rows = bass.ds(it * (2 * G * D) + hd * G * D, G * D)
                    sp.dma_start(wo_raw[:, :, :], w_o[rows, :].rearrange("(g p) n -> p g n", p=P)
                                 ).then_inc(wo_loaded, 16)

                for u in range(NU):
                    slot = u % RING
                    sp.wait_ge(w_ready, it * NU + (u + 1))
                    alone(sp)
                    sp.dma_start(w_raw[:, slot, :, :], W3[:, :, bass.ds(use_columns(u, it), P)]
                                 ).then_inc(w_loaded[slot], 16)
                    if u == 2:
                        load_wo(A)
                    if u == USE_QA1 + G:
                        load_wo(B)
            sp.wait_ge(s_done, PAIRS * UNITS * G)
            for j, m in enumerate((4, 3)):
                sp.dma_start(wmod2[:, j, :, :], wm[:, m, :, :]).then_inc(mod_loaded[m], 16)
            sp.wait_ge(proj_done, PAIRS * NG + 1)
            sp.wait_ge(wo_ready, PAIRS * 2 * G + 1)
            sp.dma_start(shifts[:, :], shift_in).then_inc(shifts_loaded, 16)

            def load_gu(c, par, width, count):
                sp.wait_ge(wf_ready, count)
                alone(sp)
                for m in range(2):
                    cols = bass.ds(c * P, width)
                    for k in range(KT):
                        src = qw[m][k * ROWS:(k + 1) * ROWS, cols]
                        sp.dma_start(q4[:, par, m, k, 0:width],
                                     src.unsqueeze(1).to_broadcast([ROWS, PACK, width])
                                     ).then_inc(gu_loaded[par], 16)
                    sp.dma_start(s4[:, par, m, :, 0:width],
                                 sc[m][:, cols].unsqueeze(0).to_broadcast([P, KT, width])
                                 ).then_inc(gu_loaded[par], 16)
                    sp.dma_start(z4[:, par, m, :, 0:width // PACK],
                                 zr[m][:, bass.ds(c * (P // PACK), width // PACK)].unsqueeze(0)
                                 .to_broadcast([P, KT, width // PACK])).then_inc(gu_loaded[par], 16)

            with sp.Fori(0, NC_FULL // 2) as it:
                for par in range(2):
                    load_gu(it * 2 + par, par, P, it * 4 + (2 * par + 2))
            load_gu(NC_FULL, 0, C_LAST, 2 * NC_FULL + 2)

            def load_down(c):
                par, rows = c % 2, (ROWS if c < NC_FULL else C_LAST // PACK)
                sp.dma_start(qd[0:rows * PACK, par, :],
                             qw[2][c * ROWS:c * ROWS + rows, :].unsqueeze(1).to_broadcast([rows, PACK, H])
                             ).then_inc(d_loaded[par], 16)
                sp.dma_start(sd[:, par, :], sc[2][c:c + 1, :].to_broadcast([P, H])
                             ).then_inc(d_loaded[par], 16)
                sp.dma_start(zd[:, par, :], zr[2][c:c + 1, :].to_broadcast([P, H // PACK])
                             ).then_inc(d_loaded[par], 16)

            sp.wait_ge(x_added, PAIRS * UNITS + 1)
            for c in range(NCH):
                if c >= 2:
                    sp.wait_ge(wf_ready, 4 + 2 * NCH + (c - 1))
                load_down(c)
            for t in range(NT):
                sp.wait_ge(fin_ready, t + 1)
                sp.dma_start(out[t * P:(t + 1) * P, :], fin[:, t % FINB, :]).then_inc(out_stored[t % FINB], 16)
            for i in range(FINB):
                sp.wait_ge(out_stored[i], 16 * (NT // FINB))

        @block.gpsimd
        def _(pool):
            pool.sem_inc(w_ready, RING)
            pool.sem_inc(act_split, 2)

            def layer_norm(n, ln_f, half):
                for k in range(half * KT + 1, (half + 1) * KT, 2):
                    tok, f = slice(k // KT * HALF, (k // KT + 1) * HALF), k % KT
                    pool.wait_ge(h_hi_done, n * 2 * KT + k + 1)
                    pool.tensor_tensor(h_lo[:, f, tok], ln_f[:, k % LNF, :], r32(h_hi[:, f, tok]),
                                       ALU.subtract).then_inc(h_lo_pool, 1)

            with pool.Fori(0, PAIRS) as it:
                def scale_wo(hd, g):
                    pool.wait_ge(wo_loaded, it * 32 + (hd + 1) * 16)
                    pool.tensor_tensor(wo_raw[:, g, :], wo_raw[:, g, :], gate_a[:, :], ALU.mult
                                       ).then_inc(wo_scaled, 1)

                def split_use(u):
                    slot = u % RING
                    pool.wait_ge(w_loaded[slot], it * (NU // RING * 16) + (u // RING + 1) * 16)
                    pool.wait_ge(proj_done, it * NG + (LAST_GROUP[u - RING] + 2 if u >= RING else 1))
                    alone(pool)
                    pool.tensor_scalar(w_hi[:, slot, :, :], w_raw[:, slot, :, :], 1.0, 1.0, ALU.mult, ALU.mult
                                       ).then_inc(w_hi_done, 1)
                    pool.wait_ge(w_hi_done, it * NU + (u + 1))
                    pool.tensor_tensor(w_lo[:, slot, :, :], w_raw[:, slot, :, :], r32(w_hi[:, slot, :, :]),
                                       ALU.subtract).then_inc(w_ready, 1)

                def normalise(hd, i, g):
                    pool.wait_ge(inv_ready, it * (UNITS * G) + ((hd * NT + i) * G + g + 1))
                    alone(pool)
                    rows = probs[:, i % 2, g, 0:(i + 1) * P]
                    pool.tensor_scalar(rows, rows, inv[:, i % 2, g:g + 1], 1.0, ALU.mult, ALU.mult
                                       ).then_inc(normed, 1)

                for u in range(USE_QA1):
                    split_use(u)
                pool.wait_ge(gate_a_ready, 1)
                for g in range(G):
                    scale_wo(A, g)
                split_use(USE_QA1)
                for g in range(G):
                    normalise(A, 0, g)
                split_use(USE_QA1 + 1)
                for hd in range(2):
                    for i in range(NT):
                        nxt = next_unit(hd, i)
                        if nxt:
                            for g in range(G):
                                normalise(*nxt, g)
                            for u in uses_of(next_unit(*nxt)):
                                split_use(u)
                        if hd == A and i >= G:
                            scale_wo(B, i - G)

            def lo_weights(it, chunk, m, width):
                par = chunk % 2
                pool.wait_ge(wf_hi, it * 4 + (2 * chunk + m + 1))
                alone(pool)
                pool.tensor_tensor(gu_lo[:, par, m, :, 0:width],
                                   wf[:, m, 0:KT * width].rearrange("p (k n) -> p k n", k=KT),
                                   r32(gu_hi[:, par, m, :, 0:width]), ALU.subtract).then_inc(wf_split, 1)

            def lo_activation(it, par, half, width):
                pool.wait_ge(act_hi, it * 4 + (2 * par + half + 1))
                alone(pool)
                rows, c, tok = slice(0, width), bass.ds(it * 2 + par, 1), slice(half * HALF, (half + 1) * HALF)
                pool.tensor_tensor(t_lo[rows, c, tok], act2[rows, half:half + 1, :], r32(t_hi[rows, c, tok]),
                                   ALU.subtract).then_inc(act_split, 1)

            for half in range(2):
                lo_weights(0, 0, half, P)
                layer_norm(1, ln_f2, half)

            def ffn_chunk(it, par, width, following):
                if following:
                    for m in range(2):
                        lo_weights(it, par + 1, m, following)
                else:
                    lo_down(0)
                for half in range(2):
                    lo_activation(it, par, half, width)

            def lo_down(c):
                n = P if c < NC_FULL else C_LAST
                pool.wait_ge(wf_hi, 2 * NCH + c + 1)
                hi, lo = d_parts(c)
                pool.tensor_tensor(lo[0:n, :], wf[0:n, c % 2, :], r32(hi[0:n, :]), ALU.subtract
                                   ).then_inc(wf_split, 1)

            with pool.Fori(0, FFN_PAIRS) as it:
                for par in range(2):
                    ffn_chunk(it, par, P, P)
            ffn_chunk(FFN_PAIRS, 0, P, P)
            ffn_chunk(FFN_PAIRS, 1, P, C_LAST)
            ffn_chunk(FFN_PAIRS + 1, 0, C_LAST, 0)
            for c in range(1, NCH):
                lo_down(c)

        @block.scalar
        def _(act):
            act.dma_start(c_col[:, :], c_in).then_inc(c_loaded, 16)
            act.dma_start(ident[:, :], ident_in).then_inc(ident_loaded, 16)
            wm = w_mod.rearrange("(k p) (m n) -> p m k n", p=P, m=6)
            for j, m in enumerate((1, 0)):
                act.dma_start(wmod[:, j, :, :], wm[:, m, :, :]).then_inc(mod_loaded[m], 16)
            act.wait_ge(c_loaded, 16)
            nc.scalar.activation(c_tmp[:, 0, :], c_col[:, :], ACT.Exp, scale=-1.0).then_inc(silu_exp, 1)

            def move_row(n, rows):
                act.wait_ge(mod_row_done, n + 1)
                nc.scalar.activation(rows[0:1, n % 2, :], ps[0:1, 4 + n % 2, :], ACT.Copy).then_inc(mod_row_moved, 1)

            def square_root(part, tiles):
                act.wait_ge(var_ready, part + 1)
                nc.scalar.activation(std[:, tiles], moments[:, tiles, 1], ACT.Sqrt, bias=eps_col[:, 0:1]
                                     ).then_inc(std_ready, 1)

            def layer_norm(n, scale_col, bias_col, ln_f):
                for k in range(2 * KT):
                    half, f = k // KT, k % KT
                    if k == 0:
                        act.wait_ge(cols_ready, n + 1)
                    act.wait_ge(xn_moved, n * NT + (half + 1) * (NT // 2))
                    if k >= LNF:
                        act.wait_ge(*h_lo_done(n, k - LNF))
                    nc.scalar.activation(ln_f[:, k % LNF, :], ps[:, LN_BANK(half, f), :], ACT.Identity,
                                         scale=mod_cols[:, scale_col, f:f + 1],
                                         bias=mod_cols[:, bias_col, f:f + 1]).then_inc(ln_f_done, 1)

            square_root(0, NORM_PARTS[0][0])
            move_row(0, mod_rows)
            act.wait_ge(x_in_sem[NT - 2], 16)
            act.dma_start(wmod[:, 2, :, :], wm[:, 2, :, :]).then_inc(mod_loaded[2], 16)
            act.dma_start(table[:, :, :, :, :], head_table).then_inc(consts_loaded, 16)
            act.dma_start(sdist[:, :], sqrt_dist).then_inc(consts_loaded, 16)
            move_row(1, mod_rows)
            square_root(1, NORM_PARTS[0][1])
            layer_norm(0, 0, 1, ln_f)

            with act.Fori(0, PAIRS) as it:
                def project_hi(kind, hd, n, half):
                    G_i = group_index(kind, hd, n, half)
                    act.wait_ge(proj_done, it * NG + (G_i + 2))
                    bank = ps[:, group_bank(G_i), :]
                    tok = slice(half * HALF, (half + 1) * HALF)
                    if kind == "q":
                        ins = nc.scalar.activation(q_hi[:, n, tok], bank, ACT.Copy,
                                                   scale=consts[:, 0, hd, n:n + 1])
                    elif kind == "k":
                        ins = nc.scalar.activation(k_hi[:, tok], bank, ACT.Copy)
                    else:
                        ins = nc.scalar.activation(v_hi[:, :, n, :],
                                                   bank[:, 0:2 * D].rearrange("p (a d) -> p a d", a=2), ACT.Copy)
                    ins.then_inc(proj_hi, 1)

                def exponential(hd, i, g):
                    n = (hd * NT + i) * G + g
                    act.wait_ge(shift_ready, it * (UNITS * G) + (n + 1))
                    rows = probs[:, i % 2, g, 0:(i + 1) * P]
                    nc.scalar.activation(rows, rows, ACT.Exp, scale=consts[:, 2, hd, g:g + 1],
                                         bias=shift[:, i % 2, g:g + 1],
                                         accum_out=rowsum[:, i % 2, g:g + 1]).then_inc(exp_done, 1)

                def split_wo_hi(hd, g):
                    act.wait_ge(y_done, it * UNITS + (hd * NT + 1))
                    act.wait_ge(wo_scaled, it * (2 * G) + (hd * G + g + 1))
                    nc.scalar.activation(wo_hi[:, g, :], wo_raw[:, g, :], ACT.Copy).then_inc(wo_hi_done, 1)

                act.wait_ge(head_consts, it + 1)
                for j, grp in enumerate(HEAD_GROUPS):
                    project_hi(*grp)
                    if j - 1 in SCORES_AFTER:
                        exponential(A, 0, SCORES_AFTER.index(j - 1))
                    for g in WO_AFTER.get(j, []):
                        split_wo_hi(A, g)
                for hd in range(2):
                    for i in range(NT):
                        nxt = next_unit(hd, i)
                        waiting = []
                        for s in slots(i):
                            if s <= i:
                                b = block_index(hd, i, s)
                                act.wait_ge(t_done, it * BLOCKS + (b + 2))
                                act.wait_ge(pv_done, it * BLOCKS + (b + 1))
                                nc.scalar.activation(pt_hi[:, b % PT, :], ps[:, T_BANK + b % 2, :], ACT.Copy
                                                     ).then_inc(pt_hi_done, 1)
                            for g in waiting:
                                exponential(*nxt, g)
                            waiting = [g for g in range(G) if nxt and score_slots(hd, i)[g] == s]
                            for g in WO_SLOTS.get((hd, i, s), []):
                                split_wo_hi(hd, g)
                            for slot, grp, _u in FILL.get((hd, i), []):
                                if slot == s:
                                    project_hi(*grp)
                        for g in waiting:
                            exponential(*nxt, g)
                        n = hd * NT + i
                        act.wait_ge(pv_done, it * BLOCKS + (block_index(hd, i, i) + 1 + PT))
                        if n < UNITS - 1:
                            act.wait_ge(y_done, it * UNITS + (n + 1))
                        nc.scalar.activation(o_parts(n)[0][:, :], ps[:, O_BANK, :], ACT.Copy
                                             ).then_inc(o_hi_done, 1)

            def hi_weights(it, chunk, m, width):
                par = chunk % 2
                act.wait_ge(wf_ready, it * 4 + (2 * chunk + m + 5))
                if chunk > 0:
                    act.wait_ge(up_done, it * 4 + (2 * chunk - 1))
                nc.scalar.activation(gu_hi[:, par, m, :, 0:width],
                                     wf[:, m, 0:KT * width].rearrange("p (k n) -> p k n", k=KT), ACT.Copy
                                     ).then_inc(wf_hi, 1)

            def ffn_chunk(it, par, width, following):
                rows, c = slice(0, width), bass.ds(it * 2 + par, 1)
                for half in range(2):
                    n = 2 * par + half
                    act.wait_ge(gate_done, it * 4 + (n + 1))
                    act.wait_ge(silu_done, it * 4 + (n + 1))
                    nc.scalar.activation(sig[rows, :], ps[rows, 2 * n, :], ACT.Sigmoid).then_inc(sig_done, 1)
                    if half == 0 and following:
                        for m in range(2):
                            hi_weights(it, par + 1, m, following)
                    elif half == 0:
                        hi_down(0)
                    act.wait_ge(act_ready, it * 4 + (n + 5))
                    alone(act)
                    nc.scalar.activation(t_hi[rows, c, half * HALF:(half + 1) * HALF], act2[rows, half:half + 1, :],
                                         ACT.Copy).then_inc(act_hi, 1)

            def hi_down(c):
                n = P if c < NC_FULL else C_LAST
                act.wait_ge(wf_ready, 4 + 2 * NCH + c + 1)
                if 2 <= c < NCH - 1:
                    act.wait_ge(d_used, c - 1)
                nc.scalar.activation(d_parts(c)[0][0:n, :], wf[0:n, c % 2, :], ACT.Copy).then_inc(wf_hi, 1)

            act.wait_ge(s_done, PAIRS * UNITS * G)
            act.dma_start(wmod2[:, 2, :, :], wm[:, 5, :, :]).then_inc(mod_loaded[5], 16)
            square_root(2, NORM_PARTS[1][0])
            move_row(2, mod_rows2)
            move_row(3, mod_rows2)
            hi_weights(0, 0, 0, P)
            layer_norm(1, 2, 3, ln_f2)
            act.wait_ge(mod_done, 4)
            nc.scalar.activation(gate_b[:, :], ps[:, GATE_B_BANK, :], ACT.Copy).then_inc(gate_row, 1)
            hi_weights(0, 0, 1, P)
            with act.Fori(0, FFN_PAIRS) as it:
                for par in range(2):
                    ffn_chunk(it, par, P, P)
            ffn_chunk(FFN_PAIRS, 0, P, P)
            ffn_chunk(FFN_PAIRS, 1, P, C_LAST)
            ffn_chunk(FFN_PAIRS + 1, 0, C_LAST, 0)
            for c in range(1, NCH):
                hi_down(c)
            for t in range(NT):
                act.wait_ge(y2_done, t + 1)
                if t >= 2:
                    act.wait_ge(fin_step, t - 1)
                nc.scalar.activation(o16[:, t % 2, :], ps[:, t, :], ACT.Copy).then_inc(o16_done, 1)

        @block.vector
        def _(dve):
            dve.sem_inc(wo_ready, 1)
            dve.sem_inc(proj_split, 1)
            dve.sem_inc(s_biased, 2)
            dve.sem_inc(pt_split, 2)
            dve.sem_inc(o_split, 1)
            dve.sem_inc(x_added, 1)
            dve.sem_inc(wf_ready, 4)
            dve.sem_inc(silu_done, 1)
            dve.sem_inc(act_ready, 4)
            dve.memset(eps_col[:, :], EPS).then_inc(silu_step, 1)

            dve.wait_ge(silu_exp, 1)
            dve.tensor_scalar(c_tmp[:, 1, :], c_tmp[:, 0, :], 1.0, None, ALU.add).then_inc(silu_step, 1)
            dve.wait_ge(silu_step, 2)
            dve.reciprocal(c_tmp[:, 2, :], c_tmp[:, 1, :]).then_inc(silu_step, 1)
            dve.wait_ge(silu_step, 3)
            dve.tensor_tensor(silu_c[:, :], c_col[:, :], c_tmp[:, 2, :], ALU.mult).then_inc(silu_step, 1)
            dve.wait_ge(silu_step, 4)
            dve.tensor_copy(silu_b[:, :, :], silu_c[:, :].unsqueeze(2).to_broadcast([P, KT, P])
                            ).then_inc(silu_ready, 1)

            def statistics(t):
                dve.bn_stats(stats[:, t, :], x[:, t, :]).then_inc(stat_step, 1)

            def aggregate(tiles, count):
                dve.wait_ge(stat_step, count)
                for t in range(tiles.start, tiles.stop):
                    dve.bn_aggr(moments[:, t, :], stats[:, t, :]).then_inc(stat_step, 1)
                count += tiles.stop - tiles.start
                dve.wait_ge(stat_step, count)
                dve.sem_inc(var_ready, 1)
                return count

            def clamp(gate, size, value, count):
                dve.scalar_tensor_tensor(out=size, in0=value, scalar=-1.0, in1=value, op0=ALU.mult, op1=ALU.max
                                         ).then_inc(gate_step, 1)
                dve.wait_ge(gate_step, count + 1)
                dve.tensor_scalar(size, size, 0.25, None, ALU.max).then_inc(gate_step, 1)
                dve.tensor_scalar(value, value, 0.0, 2.0, ALU.is_ge, ALU.mult).then_inc(gate_step, 1)
                dve.wait_ge(gate_step, count + 3)
                dve.scalar_tensor_tensor(out=gate, in0=value, scalar=-1.0, in1=size, op0=ALU.add,
                                         op1=ALU.mult).then_inc(gate_step, 1)

            def normalise_rows(n, half, xn):
                for t in range(half * 4, half * 4 + 4):
                    if t >= XNB:
                        dve.wait_ge(xn_moved, n * NT + t - XNB + 1)
                    dve.tensor_scalar(xn[:, t % XNB, :], x[:, t, :], moments[:, t, 0:1], rstd[:, t:t + 1],
                                      ALU.subtract, ALU.mult).then_inc(xn_ready, 1)

            def split_rows(n, half, ln_f):
                tok = slice(half * HALF, (half + 1) * HALF)
                for f in range(KT):
                    k = half * KT + f
                    dve.wait_ge(ln_f_done, n * 2 * KT + k + 1)
                    dve.tensor_copy(h_hi[:, f, tok], ln_f[:, k % LNF, :]).then_inc(h_hi_done, 1)
                    if n == 0 or k % 2 == 0:
                        dve.wait_ge(h_hi_done, n * 2 * KT + k + 1)
                        dve.tensor_tensor(h_lo[:, f, tok], ln_f[:, k % LNF, :], r32(h_hi[:, f, tok]),
                                          ALU.subtract).then_inc(h_lo_dve, 1)

            def inverse_std(tiles, part, count):
                dve.wait_ge(std_ready, part + 1)
                dve.reciprocal(rstd[:, tiles], std[:, tiles]).then_inc(stat_step, 1)
                dve.wait_ge(stat_step, count + 1)
                return count + 1

            count = 0
            for half in range(2):
                tiles = NORM_PARTS[0][half]
                for t in range(tiles.start, tiles.stop):
                    dve.wait_ge(x_in_sem[t], 16)
                    statistics(t)
                count = aggregate(tiles, count + 4)
                count = inverse_std(tiles, half, count)
                if half == 0:
                    normalise_rows(0, 0, xn)
            dve.wait_ge(mod_done, 1)
            dve.tensor_scalar(mod_cols[:, 0, :], ps[:, MOD_BANK, 0:KT], 1.0, None, ALU.add
                              ).then_inc(gate_step, 1)
            dve.tensor_copy(mod_cols[:, 1, :], ps[:, MOD_BANK, KT:2 * KT]).then_inc(gate_step, 1)
            dve.wait_ge(gate_step, 2)
            dve.sem_inc(cols_ready, 1)
            normalise_rows(0, 1, xn)
            split_rows(0, 0, ln_f)
            split_rows(0, 1, ln_f)
            dve.wait_ge(mod_done, 2)
            dve.tensor_copy(g_tmp[:, 0, :], ps[:, GATE_BANK, :]).then_inc(gate_row, 1)
            dve.wait_ge(gate_row, 1)
            clamp(gate_a[:, :], g_tmp[:, 1, :], g_tmp[:, 0, :], 2)
            dve.wait_ge(gate_step, 6)
            dve.sem_inc(gate_a_ready, 1)

            dve.wait_ge(consts_loaded, 32)
            with dve.Fori(0, PAIRS) as it:
                def project_lo(kind, hd, n, half):
                    G_i = group_index(kind, hd, n, half)
                    dve.wait_ge(proj_hi, it * NG + (G_i + 1))
                    bank = ps[:, group_bank(G_i), :]
                    tok = slice(half * HALF, (half + 1) * HALF)
                    if kind == "q":
                        ins = dve.scalar_tensor_tensor(out=q_lo[:, n, tok], in0=bank,
                                                       scalar=consts[:, 0, hd, n:n + 1],
                                                       in1=r32(q_hi[:, n, tok]), op0=ALU.mult, op1=ALU.subtract)
                    elif kind == "k":
                        ins = dve.tensor_tensor(k_lo[:, tok], bank, r32(k_hi[:, tok]), ALU.subtract)
                    else:
                        ins = dve.tensor_tensor(v_lo[:, :, n, :],
                                                bank[:, 0:2 * D].rearrange("p (a d) -> p a d", a=2),
                                                r32(v_hi[:, :, n, :]), ALU.subtract)
                    ins.then_inc(proj_split, 1)

                def bias_and_minimum(hd, i, g, blocks_before):
                    n = (hd * NT + i) * G + g
                    dve.wait_ge(s_done, it * (UNITS * G) + (n + 1))
                    dve.wait_ge(t_done, it * BLOCKS + (blocks_before + 1))
                    alone(dve)
                    w, wb = (i + 1) * P, score_width(i)
                    nb, bank = w // wb, 2 * (g % 2)
                    dve.tensor_tensor_reduce(
                        out=probs[:, i % 2, g, 0:w].rearrange("p (b n) -> p b n", b=nb),
                        in0=ps[:, bank:bank + nb, 0:wb],
                        in1=sdist[:, S - w:S].rearrange("p (b n) -> p b n", b=nb),
                        scale=1.0, scalar=3.0e38, op0=ALU.add, op1=ALU.min,
                        accum_out=low[:, i % 2, g:g + 1]).then_inc(s_biased, 1)
                    dve.wait_ge(s_biased, it * (UNITS * G) + (n + 3))
                    dve.tensor_tensor(shift[:, i % 2, g:g + 1], low[:, i % 2, g:g + 1],
                                      consts[:, 1, hd, g:g + 1], ALU.mult).then_inc(shift_ready, 1)

                def invert(hd, i, g):
                    dve.wait_ge(exp_done, it * (UNITS * G) + ((hd * NT + i) * G + g + 1))
                    dve.reciprocal(inv[:, i % 2, g:g + 1], rowsum[:, i % 2, g:g + 1]).then_inc(inv_ready, 1)

                def add_product(n):
                    i = n % NT
                    if n > NT:
                        dve.wait_ge(x_added, it * UNITS + (n + 1))
                        statistics(i - 1)
                    dve.wait_ge(y_done, it * UNITS + (n + 2))
                    dve.tensor_tensor(x[:, i, :], ps[:, product_bank(n), :], x[:, i, :], ALU.add
                                      ).then_inc(x_added, 1)

                dve.tensor_copy(consts[:, :, :, :], table[:, bass.ds(it, 1), :, :, :].rearrange(
                    "p a c h g -> p (a c) h g")).then_inc(head_consts, 1)
                dve.wait_ge(head_consts, it + 1)
                def split_wo_lo(hd, g):
                    dve.wait_ge(wo_hi_done, it * (2 * G) + (hd * G + g + 1))
                    dve.tensor_tensor(wo_lo[:, g, :], wo_raw[:, g, :], r32(wo_hi[:, g, :]), ALU.subtract
                                      ).then_inc(wo_ready, 1)

                for j, grp in enumerate(HEAD_GROUPS):
                    project_lo(*grp)
                    for g in WO_AFTER.get(j, []):
                        split_wo_lo(A, g)
                    if j in SCORES_AFTER:
                        bias_and_minimum(A, 0, SCORES_AFTER.index(j), 0)
                    if j - 2 in SCORES_AFTER:
                        invert(A, 0, SCORES_AFTER.index(j - 2))
                for hd in range(2):
                    for i in range(NT):
                        nxt = next_unit(hd, i)
                        waiting, exps = [], []
                        for s in slots(i):
                            fresh = [g for g in range(G) if nxt and score_slots(hd, i)[g] == s]
                            if i == 0:
                                for g in fresh:
                                    bias_and_minimum(*nxt, g, block_index(hd, i, 0))
                            if s <= i:
                                b = block_index(hd, i, s)
                                dve.wait_ge(pt_hi_done, it * BLOCKS + (b + 1))
                                dve.tensor_tensor(pt_lo[:, b % PT, :], ps[:, T_BANK + b % 2, :],
                                                  r32(pt_hi[:, b % PT, :]), ALU.subtract).then_inc(pt_split, 1)
                            if nxt:
                                if i > 0:
                                    for g in fresh:
                                        bias_and_minimum(*nxt, g, block_index(hd, i, 0))
                                for g in waiting:
                                    invert(*nxt, g)
                                waiting = fresh
                            if i == 0 and s == wo_slot(hd, i) and hd == B:
                                add_product(NT - 1)
                            for g in WO_SLOTS.get((hd, i, s), []):
                                split_wo_lo(hd, g)
                            for slot, grp, _u in FILL.get((hd, i), []):
                                if slot == s:
                                    project_lo(*grp)
                            if i > 0 and s == wo_slot(hd, i) and hd * NT + i < UNITS - 1:
                                add_product(hd * NT + i - 1)
                        for g in waiting:
                            invert(*nxt, g)
                        n = hd * NT + i
                        dve.wait_ge(o_hi_done, it * UNITS + (n + 1))
                        hi, lo = o_parts(n)
                        dve.tensor_tensor(lo[:, :], ps[:, O_BANK, :], r32(hi[:, :]), ALU.subtract
                                          ).then_inc(o_split, 1)
                add_product(UNITS - 2)
                add_product(UNITS - 1)

            def dequantise(it, n, q, z, s, w, groups, rows, loaded, count, buffer_free):
                width = q.shape[-1]
                dve.wait_ge(loaded, count)
                size = groups * width
                nv = nib[0:rows, 0:size].rearrange("p (k n) -> p k n", k=groups)
                zv = znib[0:rows, 0, 0:size]
                zm = znib[0:rows, 1, 0:size]
                dve.wait_ge(wf_ready, it * 4 + (n + 4))
                if buffer_free is not None:
                    dve.wait_ge(wf_split, buffer_free)
                alone(dve)
                dve.tensor_scalar(nv, q, shifts[0:rows, 0:1], 15, ALU.logical_shift_right, ALU.bitwise_and
                                  ).then_inc(dq_step, 1)
                z4d = z.unsqueeze(3).to_broadcast([rows, groups, width // PACK, PACK])
                sh = shifts[0:rows, 1:1 + PACK].unsqueeze(1).unsqueeze(1).to_broadcast(
                    [rows, groups, width // PACK, PACK])
                dve.tensor_tensor(zv.rearrange("p (k a b) -> p k a b", k=groups, b=PACK), z4d, sh,
                                  ALU.logical_shift_right).then_inc(dq_step, 1)
                dve.wait_ge(dq_step, it * 16 + (4 * n + 2))
                alone(dve)
                dve.tensor_scalar(zm, zv, 15, None, ALU.bitwise_and).then_inc(dq_step, 1)
                dve.wait_ge(dq_step, it * 16 + (4 * n + 3))
                dve.tensor_tensor(dif[0:rows, 0:size], nib[0:rows, 0:size], zm, ALU.subtract).then_inc(dq_step, 1)
                dve.wait_ge(dq_step, it * 16 + (4 * n + 4))
                dve.scalar_tensor_tensor(out=w[0:rows, 0:size].rearrange("p (k n) -> p k n", k=groups),
                                         in0=dif[0:rows, 0:size].rearrange("p (k n) -> p k n", k=groups),
                                         scalar=-1.0, in1=s, op0=ALU.add, op1=ALU.mult).then_inc(wf_ready, 1)

            def dequantise_gu(it, chunk, width, which=(0, 1)):
                par, loads = chunk % 2, 16 * 2 * (KT + 2)
                for m in which:
                    n = 2 * chunk + m
                    dequantise(it, n, q4[:, par, m, :, 0:width], z4[:, par, m, :, 0:width // PACK],
                               s4[:, par, m, :, 0:width], wf[:, m, :], KT, P, gu_loaded[par],
                               it * loads + (chunk // 2 + 1) * loads, it * 4 + (n - 1) if chunk > 0 else None)

            dve.wait_ge(x_added, PAIRS * UNITS + 1)
            statistics(NT - 1)
            count = aggregate(slice(0, NT), count + PAIRS * (NT - 1) + 1)
            dve.tensor_copy(silu_b2[:, :, :], silu_c[:, :].unsqueeze(2).to_broadcast([P, KT, P])
                            ).then_inc(silu_ready, 1)
            dve.wait_ge(shifts_loaded, 16)
            dequantise_gu(0, 0, P, (0,))
            inverse_std(slice(0, NT), 2, count)
            normalise_rows(1, 0, xn2)
            dve.wait_ge(mod_done, 3)
            dve.tensor_scalar(mod_cols[:, 2, :], ps[:, MOD_BANK, 0:KT], 1.0, None, ALU.add).then_inc(gate_step, 1)
            dve.tensor_copy(mod_cols[:, 3, :], ps[:, MOD_BANK, KT:2 * KT]).then_inc(gate_step, 1)
            dve.wait_ge(gate_step, 8)
            dve.sem_inc(cols_ready, 1)
            normalise_rows(1, 1, xn2)
            split_rows(1, 0, ln_f2)
            dequantise_gu(0, 0, P, (1,))
            split_rows(1, 1, ln_f2)

            def ffn_chunk(it, par, width):
                for half in range(2):
                    n = 2 * par + half
                    dve.wait_ge(sig_done, it * 4 + (n + 1))
                    dve.wait_ge(act_ready, it * 4 + (n + 4))
                    dve.tensor_tensor(act1[0:width, :], ps[0:width, 2 * n, :], sig[0:width, :], ALU.mult
                                      ).then_inc(silu_done, 1)
                    dve.wait_ge(silu_done, it * 4 + (n + 2))
                    dve.wait_ge(up_done, it * 4 + (n + 2))
                    dve.wait_ge(act_split, it * 4 + (n + 1))
                    dve.tensor_tensor(act2[0:width, half, :], ps[0:width, 2 * n + 1, :],
                                      act1[0:width, :], ALU.mult).then_inc(act_ready, 1)

            def dequantise_down(c):
                n = P if c < NC_FULL else C_LAST
                dequantise(0, 2 * NCH + c, qd[0:n, c % 2, :].unsqueeze(1), zd[0:n, c % 2, :].unsqueeze(1),
                           sd[0:n, c % 2, :].unsqueeze(1), wf[:, c % 2, :], 1, n, d_loaded[c % 2],
                           (c // 2 + 1) * 48, 2 * NCH + c - 1)

            with dve.Fori(0, FFN_PAIRS) as it:
                for par in range(2):
                    dequantise_gu(it, par + 1, P)
                    ffn_chunk(it, par, P)
            dequantise_gu(FFN_PAIRS, 1, P)
            ffn_chunk(FFN_PAIRS, 0, P)
            dequantise_gu(FFN_PAIRS, 2, C_LAST)
            ffn_chunk(FFN_PAIRS, 1, P)
            dequantise_down(0)
            ffn_chunk(FFN_PAIRS + 1, 0, C_LAST)
            for c in range(1, NCH):
                dequantise_down(c)
            dve.wait_ge(gate_row, 2)
            clamp(gate_b[:, :], gate_size[:, :], gate_b[:, :], 8)
            dve.wait_ge(gate_step, 12)
            for t in range(NT):
                dve.wait_ge(o16_done, t + 1)
                if t >= FINB:
                    dve.wait_ge(out_stored[t % FINB], 16 * (t // FINB))
                dve.tensor_tensor(fin[:, t % FINB, :], o16[:, t % 2, :], gate_b[:, :], ALU.mult).then_inc(fin_step, 1)
                dve.wait_ge(fin_step, t + 1)
                dve.tensor_tensor(fin[:, t % FINB, :], fin[:, t % FINB, :], x[:, t, :], ALU.add).then_inc(fin_ready, 1)

        @block.tensor
        def _(pe):
            pe.sem_inc(proj_done, 1)
            pe.sem_inc(t_done, 1)
            pe.sem_inc(pv_done, PT)
            pe.sem_inc(y_done, 1)
            pe.sem_inc(up_done, 1)

            def products(out_ap, terms, done=None):
                for n, (l_hi, l_lo, r_hi, r_lo) in enumerate(terms):
                    pe.matmul(out_ap, l_hi, r_hi, start=(n == 0), stop=False)
                    pe.matmul(out_ap, l_hi, r_lo, start=False, stop=False)
                    ins = pe.matmul(out_ap, l_lo, r_hi, start=False, stop=(n == len(terms) - 1))
                return ins

            def modulation_columns(w, which, rows, rows_before):
                for j, m in enumerate(which):
                    pe.wait_ge(mod_loaded[m], 16)
                    for k in range(KT):
                        ins = pe.matmul(ps[0:1, 4 + j, :], silu_c[:, k:k + 1], w[:, j, k, :],
                                        start=(k == 0), stop=(k == KT - 1))
                    ins.then_inc(mod_row_done, 1)
                for j in range(2):
                    pe.wait_ge(mod_row_moved, rows_before + j + 1)
                    for f in range(KT):
                        ins = pe.transpose(ps[:, MOD_BANK, j * KT + f:j * KT + f + 1],
                                           rows[0:1, j, f * P:(f + 1) * P], ident[0:1, 0:1])
                ins.then_inc(mod_done, 1)

            def modulation_rows(w, m, bank, silu_b):
                pe.wait_ge(mod_loaded[m], 16)
                for k in range(KT):
                    ins = pe.matmul(ps[:, bank, :], silu_b[:, k, :], w[:, 2, k, :],
                                    start=(k == 0), stop=(k == KT - 1))
                ins.then_inc(mod_done, 1)

            def transpose_rows(n, half, xn):
                for t in range(half * 4, half * 4 + 4):
                    pe.wait_ge(xn_ready, n * NT + t + 1)
                    for f in range(KT):
                        c = (t % 4) * P
                        ins = pe.transpose(ps[:, LN_BANK(half, f), c:c + P], xn[:, t % XNB, f * P:(f + 1) * P],
                                           ident[:, :])
                    ins.then_inc(xn_moved, 1)

            def wait_h(n, half):
                for k in (half * KT + KT - 2, half * KT + KT - 1):
                    pe.wait_ge(*h_lo_done(n, k))

            pe.wait_ge(ident_loaded, 16)
            for _ in range(WARM_UP):
                pe.matmul(ps[:, M_BANK, 0:P], ident[:, :], ident[:, :], start=True, stop=True)
            pe.wait_ge(silu_ready, 1)
            modulation_columns(wmod, (1, 0), mod_rows, 0)
            transpose_rows(0, 0, xn)
            pe.wait_ge(cols_ready, 1)
            transpose_rows(0, 1, xn)
            pe.wait_ge(ln_f_done, 1)
            modulation_rows(wmod, 2, GATE_BANK, silu_b)
            wait_h(0, 0)

            with pe.Fori(0, PAIRS) as it:
                def project(kind, hd, n, half, use):
                    G_i = group_index(kind, hd, n, half)
                    in_head = G_i < len(HEAD_GROUPS)
                    if G_i < 3:
                        pe.wait_ge(ln_f_done, group_bank(G_i) + 1)
                    if in_head and G_i < 2:
                        pe.wait_ge(pt_split, it * BLOCKS + 2)
                    elif in_head and G_i < 3:
                        pe.wait_ge(o_split, it * UNITS + 1)
                    elif in_head:
                        pe.wait_ge(proj_split, it * NG + (G_i - 3 + 2))
                    else:
                        pe.wait_ge(proj_split, it * NG + (G_i + 1))
                    bank = ps[:, group_bank(G_i), :]
                    tok = slice(half * HALF, (half + 1) * HALF)
                    slot = use % RING
                    if kind == "v":
                        pe.wait_ge(w_ready, it * NU + (use + 2 + RING))
                        tt = slice(n * P, (n + 1) * P)
                        ins = products(bank[:, 0:2 * D],
                                       [(h_hi[:, k, tt], h_lo[:, k, tt], w_hi[:, slot:slot + 2, k, :],
                                         w_lo[:, slot:slot + 2, k, :]) for k in range(KT)])
                    else:
                        pe.wait_ge(w_ready, it * NU + (use + 1 + RING))
                        ins = products(bank, [(w_hi[:, slot, k, :], w_lo[:, slot, k, :], h_hi[:, k, tok],
                                               h_lo[:, k, tok]) for k in range(KT)])
                    ins.then_inc(proj_done, 1)

                def score(hd, i, g):
                    n = (hd * NT + i) * G + g
                    half = i // 4
                    need = max(group_index("q", hd, g, half), group_index("k", hd, 0, half))
                    pe.wait_ge(proj_split, it * NG + (need + 2))
                    pe.wait_ge(s_biased, it * (UNITS * G) + (n + 1))
                    lo = slice(i * P, (i + 1) * P)
                    wb = score_width(i)
                    for b in range((i + 1) * P // wb):
                        keys = slice(b * wb, b * wb + max(wb, 256))
                        ins = products(ps[:, 2 * (g % 2) + b, 0:max(wb, 256)],
                                       [(q_hi[:, g, lo], q_lo[:, g, lo], k_hi[:, keys], k_lo[:, keys])])
                    ins.then_inc(s_done, 1)

                def transpose_block(hd, i, s):
                    b = block_index(hd, i, s)
                    pe.wait_ge(pt_split, it * BLOCKS + (b + 1))
                    if b < 2:
                        pe.wait_ge(proj_split, it * NG + (len(HEAD_GROUPS) + b))
                    for g in range(G):
                        if s == 0:
                            pe.wait_ge(normed, it * (UNITS * G) + ((hd * NT + i) * G + g + 1))
                        ins = pe.transpose(ps[:, T_BANK + b % 2, g * P:(g + 1) * P],
                                           probs[:, i % 2, g, s * P:(s + 1) * P], ident[:, :])
                    ins.then_inc(t_done, 1)

                def attend(hd, i, s):
                    b = block_index(hd, i, s)
                    pe.wait_ge(pt_split, it * BLOCKS + (b + 3))
                    if s == 0:
                        pe.wait_ge(o_split, it * UNITS + (hd * NT + i + 1))
                    o, v1, v2 = ps[:, O_BANK, :], v_hi[:, hd, s, :], v_lo[:, hd, s, :]
                    p1, p2 = pt_hi[:, b % PT, :], pt_lo[:, b % PT, :]
                    pe.matmul(o, v1, p1, start=(s == 0), stop=False)
                    pe.matmul(o, v1, p2, start=False, stop=False)
                    ins = pe.matmul(o, v2, p1, start=False, stop=(s == i))
                    ins.then_inc(pv_done, 1)
                    return ins

                def output_product(n, groups_before):
                    pe.wait_ge(o_split, it * UNITS + (n + 2))
                    pe.wait_ge(wo_ready, it * (2 * G) + ((n // NT + 1) * G + 1))
                    if n < UNITS - 1:
                        pe.wait_ge(x_added, it * UNITS + (n + 1))
                        pe.wait_ge(proj_split, it * NG + (groups_before + 1))
                    cols = [slice(g * P, (g + 1) * P) for g in range(G)]
                    hi, lo = o_parts(n)
                    products(ps[:, product_bank(n), :], [(hi[:, cols[g]], lo[:, cols[g]], wo_hi[:, g, :],
                                                          wo_lo[:, g, :]) for g in range(G)]).then_inc(y_done, 1)

                done = len(HEAD_GROUPS)
                for j, grp in enumerate(HEAD_GROUPS):
                    if grp == ("k", A, 0, 1):
                        wait_h(0, 1)
                    project(*grp, HEAD_USES[j])
                    if j in SCORES_AFTER:
                        score(A, 0, SCORES_AFTER.index(j))
                for hd in range(2):
                    for i in range(NT):
                        n = hd * NT + i
                        nxt = next_unit(hd, i)
                        for s in slots(i):
                            if s <= i:
                                transpose_block(hd, i, s)
                            if nxt:
                                for g in range(G):
                                    if score_slots(hd, i)[g] == s:
                                        score(*nxt, g)
                            for slot, grp, use in FILL.get((hd, i), []):
                                if slot == s:
                                    products_before = n if slot > wo_slot(hd, i) and n > 0 else max(n - 1, 0)
                                    pe.wait_ge(x_added, it * UNITS + products_before + 1)
                                    project(*grp, use)
                                    done += 1
                            if s == wo_slot(hd, i) and 0 < n < UNITS - 1:
                                output_product(n - 1, done)
                            if s >= LAG:
                                attend(hd, i, s - LAG)
                output_product(UNITS - 2, done)
                output_product(UNITS - 1, done)

            pe.wait_ge(pt_split, PAIRS * BLOCKS + 2)
            pe.wait_ge(o_split, PAIRS * UNITS + 1)
            modulation_columns(wmod2, (4, 3), mod_rows2, 2)
            transpose_rows(1, 0, xn2)
            pe.wait_ge(cols_ready, 2)
            transpose_rows(1, 1, xn2)
            pe.wait_ge(silu_ready, 2)
            pe.wait_ge(ln_f_done, 2 * KT + GATE_B_BANK + 1)
            modulation_rows(wmod2, 5, GATE_B_BANK, silu_b2)

            def gate_up(it, par, width):
                for half in range(2):
                    n = 2 * par + half
                    tok = slice(half * HALF, (half + 1) * HALF)
                    if par == 0:
                        wait_h(1, half)
                        pe.wait_ge(gate_row, 1 + half)
                    pe.wait_ge(act_ready, it * 4 + (n + 1))
                    for m, done in ((0, gate_done), (1, up_done)):
                        pe.wait_ge(wf_split, it * 4 + (2 * par + m + 1))
                        products(ps[0:width, 2 * n + m, :],
                                 [(gu_hi[:, par, m, k, 0:width], gu_lo[:, par, m, k, 0:width],
                                   h_hi[:, k, tok], h_lo[:, k, tok]) for k in range(KT)]).then_inc(done, 1)

            with pe.Fori(0, NC_FULL // 2) as it:
                for par in range(2):
                    gate_up(it, par, P)
            gate_up(NC_FULL // 2, 0, C_LAST)
            def down(c, t):
                rows = P if c < NC_FULL else C_LAST
                tok = slice(t * P, (t + 1) * P)
                l1, l2, (r1, r2) = t_hi[0:rows, c, tok], t_lo[0:rows, c, tok], (d[0:rows, :] for d in d_parts(c))
                pe.matmul(ps[:, t, :], l1, r1, start=(c == 0), stop=False)
                pe.matmul(ps[:, t, :], l1, r2, start=False, stop=False)
                return pe.matmul(ps[:, t, :], l2, r1, start=False, stop=(c == NCH - 1))

            pe.wait_ge(act_ready, 2 * NCH + 2)
            for c in range(NCH - 2):
                pe.wait_ge(wf_split, 2 * NCH + c + 1)
                for t in (4, 5, 6, 7, 0, 1, 2, 3):
                    if c == 0 and t == 0:
                        pe.wait_ge(act_ready, 2 * NCH + 4)
                    ins = down(c, t)
                ins.then_inc(d_used, 1)
            pe.wait_ge(wf_split, 3 * NCH)
            pe.wait_ge(act_split, 2 * NCH + 2)
            for t in range(NT):
                down(NCH - 2, t)
                down(NCH - 1, t).then_inc(y2_done, 1)


def kernel(**inputs):
    import numpy as _np
    import concourse.bacc as _bacc
    from concourse import mybir as _mybir
    from concourse.bass_utils import run_bass_kernel_spmd as _run

    nc = _bacc.Bacc("TRN2", target_bir_lowering=False, num_devices=1)
    arrays = {}

    def dram(name, a):
        a = _np.ascontiguousarray(a)
        arrays[name] = a
        return nc.dram_tensor(name, a.shape, _mybir.dt.from_np(a.dtype), kind="ExternalInput").ap()

    p = _np.arange(P)[:, None]
    rel = p + (S - P) - _np.arange(S)[None, :]
    sqrt_dist = _np.where(rel >= 0, _np.sqrt(_np.maximum(rel, 0).astype(_np.float32)),
                          _np.float32(MASKED)).astype(_np.float32)
    slope_base = 2.0 ** (-8.0 / NH)
    slopes = (slope_base ** _np.arange(1, NH + 1, dtype=_np.float32)).astype(_np.float32)
    per_head = slopes.reshape(PAIRS, 1, 2, G)
    table = _np.concatenate([-_np.float32(D ** -0.5) / per_head, per_head, -per_head], axis=1)
    table = _np.broadcast_to(table[None], (P,) + table.shape).astype(_np.float32)
    shifts = _np.concatenate([_np.broadcast_to(4 * (p % PACK), (P, 1)),
                              _np.broadcast_to(4 * _np.arange(PACK), (P, PACK))], axis=1).astype(_np.int32)

    args = [
        dram("x_dram", inputs["L0_attn_hidden_states"][0]),
        dram("w_qkv_dram", inputs["L0_attn_w_qkv"]),
        dram("w_o_dram", inputs["L0_attn_w_o"]),
        [dram(f"{m}_q_dram", inputs[f"L0_ffn_{m}_qweight"]) for m in ("gate", "up", "down")],
        [dram(f"{m}_s_dram", inputs[f"L0_ffn_{m}_scales"]) for m in ("gate", "up", "down")],
        [dram(f"{m}_z_dram", inputs[f"L0_ffn_{m}_zeros"]) for m in ("gate", "up", "down")],
        dram("c_dram", _np.asarray(inputs["L0_c"]).reshape(KT, P).T),
        dram("w_mod_dram", inputs["L0_wmod"]),
        dram("sqrt_dist_dram", sqrt_dist),
        dram("head_table_dram", table),
        dram("ident_dram", _np.eye(P, dtype=_np.float32)),
        dram("shifts_dram", shifts),
        nc.dram_tensor("out_dram", (S, H), F32, kind="ExternalOutput").ap(),
    ]
    build(nc, *args)
    r = _run(nc, [arrays], core_ids=[0])
    return r.results[0]["out_dram"].reshape(1, S, H)
```
